# Optimizing a Trainium2 kernel written in Bass

```python
import numpy as np
import jax
import jax.numpy as jnp

def _softmax(x, axis=-1):
    return jax.nn.softmax(x, axis=axis)

def _gelu(x):
    return jax.nn.gelu(x, approximate=True)

def _silu(x):
    return jax.nn.silu(x)

def _sigmoid(x):
    return jax.nn.sigmoid(x)

def _layernorm(x, axis=-1, eps=1e-05):
    m = jnp.mean(x, axis=axis, keepdims=True)
    v = jnp.var(x, axis=axis, keepdims=True)
    return (x - m) / jnp.sqrt(v + eps)

def _scatter_add(tgt, idx, src, axis=0):
    return tgt.at[idx].add(src)

def _segment_sum(src, seg, n):
    return jax.ops.segment_sum(src, seg, n)
kernel_name = 'mk_flamingo_gated_d4_seqx_r8_6b1b33'

def setup_inputs(seed: int=0):
    np.random.seed(seed)
    _w = jnp.asarray

    def _rec_inputs():
        import jax
        import jax.numpy as jnp
        _rk = jax.random.key(seed)
        x = -0.0003929 + 0.9999 * jax.random.normal(jax.random.fold_in(_rk, 1), (4, 256, 256), jnp.float32)
        _lenS = 256 - jax.random.randint(jax.random.fold_in(_rk, 7), (4,), 0, max(1, 256 // 4) + 1, jnp.int32)
        _lenS2 = 512 - jax.random.randint(jax.random.fold_in(_rk, 8), (4,), 0, max(1, 512 // 4) + 1, jnp.int32)
        _ctx_2048P = jax.random.normal(jax.random.fold_in(_rk, 11), (4, 16, 256), jnp.float32)
        _ctx_2048c = jax.random.dirichlet(jax.random.fold_in(_rk, 511), 0.3 * jnp.ones((16,), jnp.float32), (4, 512))
        _ctx_2048t = jnp.einsum('bsk,bkd->bsd', _ctx_2048c, _ctx_2048P)
        _ctx_2048t = _ctx_2048t * jax.lax.rsqrt(jnp.mean(jnp.square(_ctx_2048t)) + 1e-12) * 0.953939
        ctx_2048 = -0.000514642 + 1.00011 * (_ctx_2048t + 0.3 * jax.random.normal(jax.random.fold_in(_rk, 611), (4, 512, 256), jnp.float32))
        _validS = jnp.arange(256)[None, :] < _lenS[:, None]
        _validS2 = jnp.arange(512)[None, :] < _lenS2[:, None]
        _causal = jnp.tril(jnp.ones((256, 256), dtype=bool))
        mask_BxS2_ik0 = jnp.where(jnp.broadcast_to(_validS2[:, :], (4, 512)), 0, 1).astype(jnp.int32)
        mask_BxS2_bk0 = jnp.logical_not(jnp.broadcast_to(_validS2[:, :], (4, 512)))
        _g = jax.random.normal(jax.random.fold_in(_rk, 9001), (2, 4), jnp.float32)
        _g = jnp.sign(_g) * jnp.maximum(jnp.abs(_g), 1.0) + (_g == 0) * 1.0
        g_xattn = _g[0]
        g_ffn = _g[1]
        return (x, ctx_2048, mask_BxS2_ik0, mask_BxS2_bk0, g_xattn, g_ffn)
    x, ctx_2048, mask_BxS2_ik0, mask_BxS2_bk0, g_xattn, g_ffn = _rec_inputs()

    def _L0_xattn_setup():
        import jax, jax.numpy as jnp
        import numpy as np
        import math
        H = 256
        NH = 16
        HD = H // NH
        EPS_LN = 1e-05
        RES_SCALE_MAX = 0.3

        def _nan_clean(x, lim=10000.0):
            return jnp.nan_to_num(x, nan=0.0, posinf=lim, neginf=-lim)
        key = jax.random.key(seed)
        ks = jax.random.split(key, 12)
        B, S, T = (4, 256, 32)
        std = 1.0 / math.sqrt(H)
        return {'hidden_states': jax.random.normal(ks[0], (B, S, H), jnp.float32), 'audio_tokens': jax.random.normal(ks[1], (B, T, H), jnp.float32), 'attention_mask': jax.random.randint(ks[2], (B, T), 0, 2, jnp.int32), 'Wq': jax.random.normal(ks[3], (H, H), jnp.float32) * std, 'bq': jnp.zeros((H,), jnp.float32), 'Wk': jax.random.normal(ks[4], (H, H), jnp.float32) * std, 'bk': jnp.zeros((H,), jnp.float32), 'Wv': jax.random.normal(ks[5], (H, H), jnp.float32) * std, 'bv': jnp.zeros((H,), jnp.float32), 'Wo': jax.random.normal(ks[6], (H, H), jnp.float32) * std, 'bo': jnp.zeros((H,), jnp.float32), 'ln_gamma': jnp.ones((H,), jnp.float32), 'ln_beta': jnp.zeros((H,), jnp.float32), 'residual_scale': jnp.float32(0.05)}
    _L0_xattn_all = _L0_xattn_setup()
    _L0_xattn_in = {k: v for k, v in _L0_xattn_all.items() if k in ('Wq', 'bq', 'Wk', 'bk', 'Wv', 'bv', 'Wo', 'bo', 'ln_gamma', 'ln_beta', 'residual_scale')}
    del _L0_xattn_all

    def _L0_ffn_setup():
        import jax, jax.numpy as jnp
        import numpy as np
        B, L, D = (2, 128, 256)
        E, K = (8, 2)
        H, HS = (176, 352)
        key = jax.random.key(seed)
        ks = jax.random.split(key, 9)
        s = 0.02
        return {'x': jax.random.normal(ks[0], (B, L, D), dtype=jnp.float32), 'gate_w': jax.random.normal(ks[1], (E, D), dtype=jnp.float32) * s, 'w_gate': jax.random.normal(ks[2], (E, D, H), dtype=jnp.float32) * s, 'w_up': jax.random.normal(ks[3], (E, D, H), dtype=jnp.float32) * s, 'w_down': jax.random.normal(ks[4], (E, H, D), dtype=jnp.float32) * s, 'shgate_w': jax.random.normal(ks[5], (D,), dtype=jnp.float32) * s, 'shw_gate': jax.random.normal(ks[6], (D, HS), dtype=jnp.float32) * s, 'shw_up': jax.random.normal(ks[7], (D, HS), dtype=jnp.float32) * s, 'shw_down': jax.random.normal(ks[8], (HS, D), dtype=jnp.float32) * s}
    _L0_ffn_all = _L0_ffn_setup()
    _L0_ffn_in = {k: v for k, v in _L0_ffn_all.items() if k in ('gate_w', 'w_gate', 'w_up', 'w_down', 'shgate_w', 'shw_gate', 'shw_up', 'shw_down')}
    del _L0_ffn_all

    def _L1_xattn_setup():
        import jax, jax.numpy as jnp
        import numpy as np
        key = jax.random.key(seed)
        k1, k2, k3 = jax.random.split(key, 3)
        B, S, D, M = (8, 256, 256, 128)
        hidden_states = jax.random.normal(k1, (B, S, D), dtype=jnp.float32)
        memory_tokens = jax.random.normal(k2, (B, M, D), dtype=jnp.float32)
        memory_mask = jax.random.randint(k3, (B, M), 0, 2).astype(jnp.bool_)
        return {'hidden_states': hidden_states, 'memory_tokens': memory_tokens, 'memory_mask': memory_mask}
    _L1_xattn_all = _L1_xattn_setup()
    _L1_xattn_in = {k: v for k, v in _L1_xattn_all.items() if k in ()}
    del _L1_xattn_all

    def _L1_ffn_setup():
        import jax, jax.numpy as jnp
        import numpy as np
        E = 8
        TOP_K = 2
        D = 256
        F = 128
        FS = 256
        B, T = (2, 128)
        key = jax.random.key(seed)
        ks = jax.random.split(key, 8)
        s = 0.02
        return {'x': jax.random.normal(ks[0], (B, T, D), dtype=jnp.float32), 'router_w': jax.random.normal(ks[1], (D, E), dtype=jnp.float32) * s, 'shared_gate': jax.random.normal(ks[2], (D, FS), dtype=jnp.float32) * s, 'shared_up': jax.random.normal(ks[3], (D, FS), dtype=jnp.float32) * s, 'shared_down': jax.random.normal(ks[4], (FS, D), dtype=jnp.float32) * s, 'w_gate': jax.random.normal(ks[5], (E, D, F), dtype=jnp.float32) * s, 'w_up': jax.random.normal(ks[6], (E, D, F), dtype=jnp.float32) * s, 'w_down': jax.random.normal(ks[7], (E, F, D), dtype=jnp.float32) * s}
    _L1_ffn_all = _L1_ffn_setup()
    _L1_ffn_in = {k: v for k, v in _L1_ffn_all.items() if k in ('router_w', 'shared_gate', 'shared_up', 'shared_down', 'w_gate', 'w_up', 'w_down')}
    del _L1_ffn_all

    def _L2_xattn_setup():
        import jax, jax.numpy as jnp
        import numpy as np
        NUM_HEADS = 16

        def _qdq(x):
            s = jnp.maximum(jnp.max(jnp.abs(x), axis=-1, keepdims=True) / 127.0, 1e-08)
            return jnp.clip(jnp.round(x / s), -127.0, 127.0) * s
        key = jax.random.key(seed)
        ks = jax.random.split(key, 8)
        B, N, M, D = (2, 512, 64, 256)
        w_std = 0.02
        return {'x': jax.random.normal(ks[0], (B, N, D), jnp.float32), 'cond': jax.random.normal(ks[1], (B, M, D), jnp.float32), 'wq': jax.random.normal(ks[2], (D, D), jnp.float32) * w_std, 'bq': jax.random.normal(ks[3], (D,), jnp.float32) * w_std, 'wkv': jax.random.normal(ks[4], (2 * D, D), jnp.float32) * w_std, 'bkv': jax.random.normal(ks[5], (2 * D,), jnp.float32) * w_std, 'wp': jax.random.normal(ks[6], (D, D), jnp.float32) * w_std, 'bp': jax.random.normal(ks[7], (D,), jnp.float32) * w_std}
    _L2_xattn_all = _L2_xattn_setup()
    _L2_xattn_in = {k: v for k, v in _L2_xattn_all.items() if k in ('wq', 'bq', 'wkv', 'bkv', 'wp', 'bp')}
    del _L2_xattn_all

    def _L2_ffn_setup():
        import jax, jax.numpy as jnp
        import numpy as np

        @jax.custom_vjp
        def ste_sign(x):
            return jnp.sign(x)

        def _ste_fwd(x):
            return (jnp.sign(x), None)

        def _ste_bwd(_, g):
            return (g,)
        ste_sign.defvjp(_ste_fwd, _ste_bwd)
        D_MODEL = 256
        D_HIDDEN = 1024
        key = jax.random.key(seed)
        k_x, k_up, k_dn = jax.random.split(key, 3)
        x = jax.random.normal(k_x, (2, 256, D_MODEL), dtype=jnp.float32)
        up_weight = jax.random.normal(k_up, (D_HIDDEN, D_MODEL), dtype=jnp.float32) * 0.02
        down_weight = jax.random.normal(k_dn, (D_MODEL, D_HIDDEN), dtype=jnp.float32) * 0.02
        up_scale = jnp.ones((D_HIDDEN,), dtype=jnp.float32)
        down_scale = jnp.ones((D_MODEL,), dtype=jnp.float32)
        output_scale = jnp.ones((1,), dtype=jnp.float32)
        return {'x': x, 'up_weight': up_weight, 'down_weight': down_weight, 'up_scale': up_scale, 'down_scale': down_scale, 'output_scale': output_scale}
    _L2_ffn_all = _L2_ffn_setup()
    _L2_ffn_in = {k: v for k, v in _L2_ffn_all.items() if k in ('up_weight', 'down_weight', 'up_scale', 'down_scale', 'output_scale')}
    del _L2_ffn_all

    def _L3_xattn_setup():
        import jax, jax.numpy as jnp
        import numpy as np
        DIM = 256
        N_HEADS = 16
        HEAD_DIM = DIM // N_HEADS
        EPS = 1e-06
        IMG_LEN = 257

        def rms_norm(x, g, eps=EPS):
            var = jnp.mean(x * x, axis=-1, keepdims=True)
            return x * jax.lax.rsqrt(var + eps) * g

        def _attend(q, k, v, k_mask=None):
            scale = 1.0 / jnp.sqrt(jnp.asarray(HEAD_DIM, q.dtype))
            scores = jnp.einsum('bqnd,bknd->bnqk', q, k) * scale
            if k_mask is not None:
                neg = jnp.asarray(jnp.finfo(scores.dtype).min, scores.dtype)
                scores = jnp.where(k_mask[:, None, None, :], scores, neg)
            probs = jax.nn.softmax(scores, axis=-1)
            return jnp.einsum('bnqk,bknd->bqnd', probs, v)
        key = jax.random.key(seed)
        ks = jax.random.split(key, 16)
        B, L1, L2 = (1, 2048, 769)
        std = 0.02
        inp = {'x': jax.random.normal(ks[0], (B, L1, DIM), jnp.float32), 'context': jax.random.normal(ks[1], (B, L2, DIM), jnp.float32), 'context_lens': jax.random.randint(ks[2], (B,), 32, 513, jnp.int32), 'Wq': jax.random.normal(ks[3], (DIM, DIM), jnp.float32) * std, 'bq': jnp.zeros((DIM,), jnp.float32), 'gq': jnp.ones((DIM,), jnp.float32), 'Wk': jax.random.normal(ks[4], (DIM, DIM), jnp.float32) * std, 'bk': jnp.zeros((DIM,), jnp.float32), 'gk': jnp.ones((DIM,), jnp.float32), 'Wv': jax.random.normal(ks[5], (DIM, DIM), jnp.float32) * std, 'bv': jnp.zeros((DIM,), jnp.float32), 'Wk_img': jax.random.normal(ks[6], (DIM, DIM), jnp.float32) * std, 'bk_img': jnp.zeros((DIM,), jnp.float32), 'gk_img': jnp.ones((DIM,), jnp.float32), 'Wv_img': jax.random.normal(ks[7], (DIM, DIM), jnp.float32) * std, 'bv_img': jnp.zeros((DIM,), jnp.float32), 'Wo': jax.random.normal(ks[8], (DIM, DIM), jnp.float32) * std, 'bo': jnp.zeros((DIM,), jnp.float32)}
        return inp
    _L3_xattn_all = _L3_xattn_setup()
    _L3_xattn_in = {k: v for k, v in _L3_xattn_all.items() if k in ('context_lens', 'Wq', 'bq', 'gq', 'Wk', 'bk', 'gk', 'Wv', 'bv', 'Wk_img', 'bk_img', 'gk_img', 'Wv_img', 'bv_img', 'Wo', 'bo')}
    del _L3_xattn_all

    def _L3_ffn_setup():
        import jax, jax.numpy as jnp
        import numpy as np
        H, I, E, TOP_K = (256, 176, 16, 6)
        IS = 352
        NORM_TOPK_PROB = False

        def _silu_and_mul(gate_up):
            d = gate_up.shape[-1] // 2
            g, u = (gate_up[..., :d], gate_up[..., d:])
            return jax.nn.silu(g) * u
        key = jax.random.key(seed)
        ks = jax.random.split(key, 6)
        s = 0.02
        return {'x': jax.random.normal(ks[0], (1, 256, H), jnp.float32), 'gate_w': jax.random.normal(ks[1], (E, H), jnp.float32) * s, 'w1': jax.random.normal(ks[2], (E, 2 * I, H), jnp.float32) * s, 'w2': jax.random.normal(ks[3], (E, H, I), jnp.float32) * s, 'shared_w1': jax.random.normal(ks[4], (2 * IS, H), jnp.float32) * s, 'shared_w2': jax.random.normal(ks[5], (H, IS), jnp.float32) * s}
    _L3_ffn_all = _L3_ffn_setup()
    _L3_ffn_in = {k: v for k, v in _L3_ffn_all.items() if k in ('gate_w', 'w1', 'w2', 'shared_w1', 'shared_w2')}
    del _L3_ffn_all
    return {'x': x, 'ctx_2048': ctx_2048, 'mask_BxS2_ik0': mask_BxS2_ik0, 'mask_BxS2_bk0': mask_BxS2_bk0, 'g_xattn': g_xattn, 'g_ffn': g_ffn, 'L0_xattn_Wq': _L0_xattn_in['Wq'], 'L0_xattn_bq': _L0_xattn_in['bq'], 'L0_xattn_Wk': _L0_xattn_in['Wk'], 'L0_xattn_bk': _L0_xattn_in['bk'], 'L0_xattn_Wv': _L0_xattn_in['Wv'], 'L0_xattn_bv': _L0_xattn_in['bv'], 'L0_xattn_Wo': _L0_xattn_in['Wo'], 'L0_xattn_bo': _L0_xattn_in['bo'], 'L0_xattn_ln_gamma': _L0_xattn_in['ln_gamma'], 'L0_xattn_ln_beta': _L0_xattn_in['ln_beta'], 'L0_xattn_residual_scale': _L0_xattn_in['residual_scale'], 'L0_ffn_gate_w': _L0_ffn_in['gate_w'], 'L0_ffn_w_gate': _L0_ffn_in['w_gate'], 'L0_ffn_w_up': _L0_ffn_in['w_up'], 'L0_ffn_w_down': _L0_ffn_in['w_down'], 'L0_ffn_shgate_w': _L0_ffn_in['shgate_w'], 'L0_ffn_shw_gate': _L0_ffn_in['shw_gate'], 'L0_ffn_shw_up': _L0_ffn_in['shw_up'], 'L0_ffn_shw_down': _L0_ffn_in['shw_down'], 'L1_ffn_router_w': _L1_ffn_in['router_w'], 'L1_ffn_shared_gate': _L1_ffn_in['shared_gate'], 'L1_ffn_shared_up': _L1_ffn_in['shared_up'], 'L1_ffn_shared_down': _L1_ffn_in['shared_down'], 'L1_ffn_w_gate': _L1_ffn_in['w_gate'], 'L1_ffn_w_up': _L1_ffn_in['w_up'], 'L1_ffn_w_down': _L1_ffn_in['w_down'], 'L2_xattn_wq': _L2_xattn_in['wq'], 'L2_xattn_bq': _L2_xattn_in['bq'], 'L2_xattn_wkv': _L2_xattn_in['wkv'], 'L2_xattn_bkv': _L2_xattn_in['bkv'], 'L2_xattn_wp': _L2_xattn_in['wp'], 'L2_xattn_bp': _L2_xattn_in['bp'], 'L2_ffn_up_weight': _L2_ffn_in['up_weight'], 'L2_ffn_down_weight': _L2_ffn_in['down_weight'], 'L2_ffn_up_scale': _L2_ffn_in['up_scale'], 'L2_ffn_down_scale': _L2_ffn_in['down_scale'], 'L2_ffn_output_scale': _L2_ffn_in['output_scale'], 'L3_xattn_context_lens': _L3_xattn_in['context_lens'], 'L3_xattn_Wq': _L3_xattn_in['Wq'], 'L3_xattn_bq': _L3_xattn_in['bq'], 'L3_xattn_gq': _L3_xattn_in['gq'], 'L3_xattn_Wk': _L3_xattn_in['Wk'], 'L3_xattn_bk': _L3_xattn_in['bk'], 'L3_xattn_gk': _L3_xattn_in['gk'], 'L3_xattn_Wv': _L3_xattn_in['Wv'], 'L3_xattn_bv': _L3_xattn_in['bv'], 'L3_xattn_Wk_img': _L3_xattn_in['Wk_img'], 'L3_xattn_bk_img': _L3_xattn_in['bk_img'], 'L3_xattn_gk_img': _L3_xattn_in['gk_img'], 'L3_xattn_Wv_img': _L3_xattn_in['Wv_img'], 'L3_xattn_bv_img': _L3_xattn_in['bv_img'], 'L3_xattn_Wo': _L3_xattn_in['Wo'], 'L3_xattn_bo': _L3_xattn_in['bo'], 'L3_ffn_gate_w': _L3_ffn_in['gate_w'], 'L3_ffn_w1': _L3_ffn_in['w1'], 'L3_ffn_w2': _L3_ffn_in['w2'], 'L3_ffn_shared_w1': _L3_ffn_in['shared_w1'], 'L3_ffn_shared_w2': _L3_ffn_in['shared_w2']}

def reference(x, ctx_2048, mask_BxS2_ik0, mask_BxS2_bk0, g_xattn, g_ffn, L0_xattn_Wq, L0_xattn_bq, L0_xattn_Wk, L0_xattn_bk, L0_xattn_Wv, L0_xattn_bv, L0_xattn_Wo, L0_xattn_bo, L0_xattn_ln_gamma, L0_xattn_ln_beta, L0_xattn_residual_scale, L0_ffn_gate_w, L0_ffn_w_gate, L0_ffn_w_up, L0_ffn_w_down, L0_ffn_shgate_w, L0_ffn_shw_gate, L0_ffn_shw_up, L0_ffn_shw_down, L1_ffn_router_w, L1_ffn_shared_gate, L1_ffn_shared_up, L1_ffn_shared_down, L1_ffn_w_gate, L1_ffn_w_up, L1_ffn_w_down, L2_xattn_wq, L2_xattn_bq, L2_xattn_wkv, L2_xattn_bkv, L2_xattn_wp, L2_xattn_bp, L2_ffn_up_weight, L2_ffn_down_weight, L2_ffn_up_scale, L2_ffn_down_scale, L2_ffn_output_scale, L3_xattn_context_lens, L3_xattn_Wq, L3_xattn_bq, L3_xattn_gq, L3_xattn_Wk, L3_xattn_bk, L3_xattn_gk, L3_xattn_Wv, L3_xattn_bv, L3_xattn_Wk_img, L3_xattn_bk_img, L3_xattn_gk_img, L3_xattn_Wv_img, L3_xattn_bv_img, L3_xattn_Wo, L3_xattn_bo, L3_ffn_gate_w, L3_ffn_w1, L3_ffn_w2, L3_ffn_shared_w1, L3_ffn_shared_w2):
    import jax
    import jax.numpy as jnp

    def _L0_xattn_ref(hidden_states, audio_tokens, attention_mask, Wq, bq, Wk, bk, Wv, bv, Wo, bo, ln_gamma, ln_beta, residual_scale):
        import jax, jax.numpy as jnp
        import numpy as np
        import math
        H = 256
        NH = 16
        HD = H // NH
        EPS_LN = 1e-05
        RES_SCALE_MAX = 0.3

        def _nan_clean(x, lim=10000.0):
            return jnp.nan_to_num(x, nan=0.0, posinf=lim, neginf=-lim)
        B, S, _ = hidden_states.shape
        T = audio_tokens.shape[1]
        hs = _nan_clean(hidden_states).astype(jnp.float32)
        at = _nan_clean(audio_tokens).astype(jnp.float32)

        def proj(x, W, b, L):
            y = x @ W.T + b
            return y.reshape(B, L, NH, HD).transpose(0, 2, 1, 3)
        q = _nan_clean(proj(hs, Wq, bq, S))
        k = _nan_clean(proj(at, Wk, bk, T))
        v = _nan_clean(proj(at, Wv, bv, T))
        scale = max(math.sqrt(HD), 1e-08)
        scores = jnp.einsum('bhsd,bhtd->bhst', q, k) / scale
        scores = jnp.clip(scores, -50.0, 50.0)
        scores = jnp.nan_to_num(scores, nan=0.0, posinf=50.0, neginf=-50.0)
        attend = (attention_mask.astype(jnp.float32) > 0.5)[:, None, None, :]
        scores = jnp.where(attend, scores, -10000.0)
        scores = jnp.clip(scores, -50.0, 50.0)
        probs = jax.nn.softmax(scores, axis=-1)
        probs = jnp.nan_to_num(probs, nan=0.0, posinf=1.0, neginf=0.0)
        probs = probs / (probs.sum(axis=-1, keepdims=True) + 1e-08)
        ctx = jnp.einsum('bhst,bhtd->bhsd', probs, v)
        ctx = ctx.transpose(0, 2, 1, 3).reshape(B, S, H)
        delta = _nan_clean(ctx @ Wo.T + bo)
        rs = jnp.clip(residual_scale, 0.0, RES_SCALE_MAX)
        delta = rs * delta
        mu = delta.mean(axis=-1, keepdims=True)
        var = jnp.mean((delta - mu) ** 2, axis=-1, keepdims=True)
        delta = (delta - mu) / jnp.sqrt(var + EPS_LN) * ln_gamma + ln_beta
        return delta

    def _L0_ffn_ref(x, gate_w, w_gate, w_up, w_down, shgate_w, shw_gate, shw_up, shw_down):
        import jax, jax.numpy as jnp
        import numpy as np
        B, L, D = (2, 128, 256)
        E, K = (8, 2)
        H, HS = (176, 352)
        b, l, d = x.shape
        xf = x.reshape(-1, d)
        logits = jnp.einsum('td,ed->te', xf.astype(jnp.float32), gate_w)
        probs = jax.nn.softmax(logits.astype(jnp.float32), axis=-1)
        weights, indices = jax.lax.top_k(probs, K)
        weights = (weights / weights.sum(-1, keepdims=True)).astype(x.dtype)
        onehot = jax.nn.one_hot(indices, E, dtype=x.dtype)
        combine = jnp.einsum('tk,tke->te', weights, onehot)
        g = jnp.einsum('td,edh->teh', xf, w_gate)
        u = jnp.einsum('td,edh->teh', xf, w_up)
        h = jax.nn.silu(g) * u
        out = jnp.einsum('teh,ehd,te->td', h.astype(jnp.float32), w_down.astype(jnp.float32), combine.astype(jnp.float32))
        sgate = jax.nn.sigmoid(xf @ shgate_w)[:, None]
        sh = jax.nn.silu(xf @ shw_gate) * (xf @ shw_up) @ shw_down
        out = out + (sgate * sh).astype(jnp.float32)
        return out.astype(x.dtype).reshape(b, l, d)

    def _L1_xattn_ref(hidden_states, memory_tokens, memory_mask):
        import jax, jax.numpy as jnp
        import numpy as np
        B, S, D = hidden_states.shape
        scale = 1.0 / jnp.sqrt(jnp.asarray(D, hidden_states.dtype))
        scores = jnp.einsum('bsd,bmd->bsm', hidden_states, memory_tokens) * scale
        neg_inf = jnp.asarray(-1e+30, scores.dtype)
        scores = jnp.where(memory_mask[:, None, :], scores, neg_inf)
        attn = jax.nn.softmax(scores, axis=-1)
        readout = jnp.einsum('bsm,bmd->bsd', attn, memory_tokens)
        valid_b = jnp.any(memory_mask, axis=-1)
        out = jnp.where(valid_b[:, None, None], readout, jnp.zeros_like(readout))
        return out

    def _L1_ffn_ref(x, router_w, shared_gate, shared_up, shared_down, w_gate, w_up, w_down):
        import jax, jax.numpy as jnp
        import numpy as np
        E = 8
        TOP_K = 2
        D = 256
        F = 128
        FS = 256
        B, T = (2, 128)
        Bx, Tx, Dx = x.shape
        N = Bx * Tx
        xf = x.reshape(N, Dx)
        shared = jax.nn.silu(xf @ shared_gate) * (xf @ shared_up) @ shared_down
        probs = jax.nn.softmax(xf @ router_w, axis=-1)
        topk_vals, topk_ids = jax.lax.top_k(probs, TOP_K)
        combine = jnp.zeros((N, E), dtype=xf.dtype).at[jnp.arange(N)[:, None], topk_ids].add(topk_vals)
        gated = jax.nn.silu(jnp.einsum('nd,edf->enf', xf, w_gate))
        up = jnp.einsum('nd,edf->enf', xf, w_up)
        y = jnp.einsum('enf,efd->end', gated * up, w_down)
        routed = jnp.einsum('ne,end->nd', combine, y)
        return (shared + routed).reshape(Bx, Tx, Dx)

    def _L2_xattn_ref(x, cond, wq, bq, wkv, bkv, wp, bp):
        import jax, jax.numpy as jnp
        import numpy as np
        NUM_HEADS = 16

        def _qdq(x):
            s = jnp.maximum(jnp.max(jnp.abs(x), axis=-1, keepdims=True) / 127.0, 1e-08)
            return jnp.clip(jnp.round(x / s), -127.0, 127.0) * s
        B, N, C = x.shape
        M = cond.shape[1]
        H = NUM_HEADS
        Dh = C // H
        q = _qdq(x) @ _qdq(wq).T + bq
        kv = cond @ wkv.T + bkv
        k, v = jnp.split(kv, 2, axis=-1)
        q = q.reshape(B, N, H, Dh)
        k = k.reshape(B, M, H, Dh)
        v = v.reshape(B, M, H, Dh)
        scale = 1.0 / np.sqrt(Dh)
        attn = jax.nn.softmax(jnp.einsum('bnhd,bmhd->bhnm', q, k) * scale, axis=-1)
        o = jnp.einsum('bhnm,bmhd->bnhd', attn, v).reshape(B, N, C)
        out = _qdq(o) @ _qdq(wp).T + bp
        return out

    def _L2_ffn_ref(x, up_weight, down_weight, up_scale, down_scale, output_scale):
        import jax, jax.numpy as jnp
        import numpy as np

        @jax.custom_vjp
        def ste_sign(x):
            return jnp.sign(x)

        def _ste_fwd(x):
            return (jnp.sign(x), None)

        def _ste_bwd(_, g):
            return (g,)
        ste_sign.defvjp(_ste_fwd, _ste_bwd)
        D_MODEL = 256
        D_HIDDEN = 1024
        up_w = ste_sign(up_weight)
        down_w = ste_sign(down_weight)
        hidden = jnp.einsum('bsd,hd->bsh', x, up_w) * up_scale
        hidden = jax.nn.relu(hidden)
        out = jnp.einsum('bsh,dh->bsd', hidden, down_w) * down_scale
        return out * output_scale

    def _L3_xattn_ref(x, context, context_lens, Wq, bq, gq, Wk, bk, gk, Wv, bv, Wk_img, bk_img, gk_img, Wv_img, bv_img, Wo, bo):
        import jax, jax.numpy as jnp
        import numpy as np
        DIM = 256
        N_HEADS = 16
        HEAD_DIM = DIM // N_HEADS
        EPS = 1e-06
        IMG_LEN = 257

        def rms_norm(x, g, eps=EPS):
            var = jnp.mean(x * x, axis=-1, keepdims=True)
            return x * jax.lax.rsqrt(var + eps) * g

        def _attend(q, k, v, k_mask=None):
            scale = 1.0 / jnp.sqrt(jnp.asarray(HEAD_DIM, q.dtype))
            scores = jnp.einsum('bqnd,bknd->bnqk', q, k) * scale
            if k_mask is not None:
                neg = jnp.asarray(jnp.finfo(scores.dtype).min, scores.dtype)
                scores = jnp.where(k_mask[:, None, None, :], scores, neg)
            probs = jax.nn.softmax(scores, axis=-1)
            return jnp.einsum('bnqk,bknd->bqnd', probs, v)
        b = x.shape[0]
        n, d = (N_HEADS, HEAD_DIM)
        ctx_img = context[:, :IMG_LEN]
        ctx_txt = context[:, IMG_LEN:]
        q = rms_norm(x @ Wq + bq, gq).reshape(b, -1, n, d)
        k = rms_norm(ctx_txt @ Wk + bk, gk).reshape(b, -1, n, d)
        v = (ctx_txt @ Wv + bv).reshape(b, -1, n, d)
        k_img = rms_norm(ctx_img @ Wk_img + bk_img, gk_img).reshape(b, -1, n, d)
        v_img = (ctx_img @ Wv_img + bv_img).reshape(b, -1, n, d)
        img_x = _attend(q, k_img, v_img)
        k_mask = jnp.arange(k.shape[1])[None, :] < context_lens[:, None]
        txt_x = _attend(q, k, v, k_mask)
        out = (txt_x + img_x).reshape(b, -1, n * d)
        return out @ Wo + bo

    def _L3_ffn_ref(x, gate_w, w1, w2, shared_w1, shared_w2):
        import jax, jax.numpy as jnp
        import numpy as np
        H, I, E, TOP_K = (256, 176, 16, 6)
        IS = 352
        NORM_TOPK_PROB = False

        def _silu_and_mul(gate_up):
            d = gate_up.shape[-1] // 2
            g, u = (gate_up[..., :d], gate_up[..., d:])
            return jax.nn.silu(g) * u
        B, S, Hd = x.shape
        xf = x.reshape(-1, Hd)
        T = xf.shape[0]
        shared_out = _silu_and_mul(xf @ shared_w1.T) @ shared_w2.T
        logits = xf @ gate_w.T
        probs = jax.nn.softmax(logits.astype(jnp.float32), axis=-1)
        routing_weights, selected = jax.lax.top_k(probs, TOP_K)
        if NORM_TOPK_PROB:
            routing_weights = routing_weights / routing_weights.sum(-1, keepdims=True)
        combine = jnp.zeros((T, E), jnp.float32).at[jnp.arange(T)[:, None], selected].add(routing_weights).astype(x.dtype)
        gate_up = jnp.einsum('th,eoh->teo', xf, w1)
        act = _silu_and_mul(gate_up)
        moe_out = jnp.einsum('te,tei,ehi->th', combine, act, w2)
        return (moe_out + shared_out).reshape(B, S, Hd)
    x = x + jnp.tanh(g_xattn[0]) * _L0_xattn_ref(_layernorm(x, axis=-1), ctx_2048, mask_BxS2_ik0, L0_xattn_Wq, L0_xattn_bq, L0_xattn_Wk, L0_xattn_bk, L0_xattn_Wv, L0_xattn_bv, L0_xattn_Wo, L0_xattn_bo, L0_xattn_ln_gamma, L0_xattn_ln_beta, L0_xattn_residual_scale)
    x = x + jnp.tanh(g_ffn[0]) * _L0_ffn_ref(_layernorm(x, axis=-1), L0_ffn_gate_w, L0_ffn_w_gate, L0_ffn_w_up, L0_ffn_w_down, L0_ffn_shgate_w, L0_ffn_shw_gate, L0_ffn_shw_up, L0_ffn_shw_down)
    x = x + jnp.tanh(g_xattn[1]) * _L1_xattn_ref(_layernorm(x, axis=-1), ctx_2048, mask_BxS2_bk0)
    x = x + jnp.tanh(g_ffn[1]) * _L1_ffn_ref(_layernorm(x, axis=-1), L1_ffn_router_w, L1_ffn_shared_gate, L1_ffn_shared_up, L1_ffn_shared_down, L1_ffn_w_gate, L1_ffn_w_up, L1_ffn_w_down)
    x = x + jnp.tanh(g_xattn[2]) * _L2_xattn_ref(_layernorm(x, axis=-1), ctx_2048, L2_xattn_wq, L2_xattn_bq, L2_xattn_wkv, L2_xattn_bkv, L2_xattn_wp, L2_xattn_bp)
    x = x + jnp.tanh(g_ffn[2]) * _L2_ffn_ref(_layernorm(x, axis=-1), L2_ffn_up_weight, L2_ffn_down_weight, L2_ffn_up_scale, L2_ffn_down_scale, L2_ffn_output_scale)
    x = x + jnp.tanh(g_xattn[3]) * _L3_xattn_ref(_layernorm(x, axis=-1), ctx_2048, L3_xattn_context_lens, L3_xattn_Wq, L3_xattn_bq, L3_xattn_gq, L3_xattn_Wk, L3_xattn_bk, L3_xattn_gk, L3_xattn_Wv, L3_xattn_bv, L3_xattn_Wk_img, L3_xattn_bk_img, L3_xattn_gk_img, L3_xattn_Wv_img, L3_xattn_bv_img, L3_xattn_Wo, L3_xattn_bo)
    x = x + jnp.tanh(g_ffn[3]) * _L3_ffn_ref(_layernorm(x, axis=-1), L3_ffn_gate_w, L3_ffn_w1, L3_ffn_w2, L3_ffn_shared_w1, L3_ffn_shared_w2)
    return x

_drawn_inputs = setup_inputs


def setup_inputs(seed=0):
    import zlib

    import numpy as np

    out = dict(_drawn_inputs(seed))
    spreads = {'L0_xattn_bq': (0.0, 0.371),
     'L0_xattn_bk': (0.0, 2.0),
     'L0_xattn_bv': (0.0, 0.1),
     'L0_xattn_bo': (0.0, 0.1),
     'L0_xattn_ln_gamma': (1.0, 0.2),
     'L0_xattn_ln_beta': (0.0, 0.1),
     'L2_ffn_up_scale': (1.0, 0.2),
     'L2_ffn_down_scale': (1.0, 0.2),
     'L3_xattn_bq': (0.0, 2.0),
     'L3_xattn_gq': (1.0, 0.6),
     'L3_xattn_bk': (0.0, 2.0),
     'L3_xattn_gk': (1.0, 0.6),
     'L3_xattn_bv': (0.0, 2.0),
     'L3_xattn_bk_img': (0.0, 2.0),
     'L3_xattn_gk_img': (1.0, 0.6),
     'L3_xattn_bv_img': (0.0, 2.0),
     'L3_xattn_bo': (0.0, 2.0)}
    factors = {'g_ffn': 8.0,
     'L0_ffn_gate_w': 8.0,
     'L0_ffn_w_gate': 8.0,
     'L0_ffn_w_up': 8.0,
     'L0_ffn_w_down': 8.0,
     'L0_ffn_shgate_w': 8.0,
     'L0_ffn_shw_gate': 8.0,
     'L0_ffn_shw_up': 8.0,
     'L0_ffn_shw_down': 8.0,
     'L1_ffn_router_w': 8.0,
     'L1_ffn_shared_gate': 5.185,
     'L1_ffn_shared_up': 5.059,
     'L1_ffn_shared_down': 4.999,
     'L1_ffn_w_gate': 8.0,
     'L1_ffn_w_up': 8.0,
     'L1_ffn_w_down': 8.0,
     'L2_xattn_wq': 64.0,
     'L2_xattn_bq': 64.0,
     'L2_xattn_bkv': 64.0,
     'L2_xattn_bp': 41.536,
     'L3_xattn_Wq': 64.0,
     'L3_xattn_Wk': 64.0,
     'L3_xattn_Wv': 60.981,
     'L3_xattn_Wk_img': 64.0,
     'L3_xattn_Wv_img': 60.263,
     'L3_xattn_Wo': 37.693,
     'L3_ffn_gate_w': 30.441,
     'L3_ffn_w1': 29.455,
     'L3_ffn_w2': 29.238,
     'L3_ffn_shared_w1': 8.0,
     'L3_ffn_shared_w2': 8.0,
     'L2_xattn_wkv': 8.0,
     'L2_xattn_wp': 8.0}
    for name, (base, spread) in spreads.items():
        noise = np.random.default_rng([zlib.crc32(name.encode()), seed]).standard_normal(out[name].shape)
        drawn = base * np.exp(spread * noise) if base else spread * noise
        out[name] = jnp.asarray(drawn.astype(out[name].dtype))
    for name, factor in factors.items():
        out[name] = (out[name] * factor).astype(out[name].dtype)
    return out
```

```python
from contextlib import ExitStack

import numpy as np

import concourse.bass as bass
from concourse import mybir

F32 = mybir.dt.float32
F32R = mybir.dt.float32r
I32 = mybir.dt.int32
U8 = mybir.dt.uint8
ACT = mybir.ActivationFunctionType
ALU = mybir.AluOpType
AX = mybir.AxisListType

P = 128
D = 256
KC = D // P
B = 4
S = 256
M = 512
T = B * S // P
QT = S // P
KT = M // P
NH = 16
HD = D // NH
NP = NH // 2
G = NH // 4
VW = HD + 1
IMG = 257
HALF = 512
SCALE = 1.0 / HD ** 0.5
EXP50P = float(np.exp(np.float64(50.0)))
EXP50N = float(np.exp(np.float64(-50.0)))
FAR = -float(2.0 ** 100)
MAGIC = 12582912.0
LN_EPS = 1e-5
RMS_EPS = 1e-6

FFN = [dict(E=8, K=2, H=176, HS=352), dict(E=8, K=2, H=128, HS=256), None,
       dict(E=16, K=6, H=176, HS=352)]
UNITS = [f["E"] * f["H"] + f["HS"] if f else 1024 for f in FFN]
TILES = [-(-u // P) for u in UNITS]
ROUTED = [0, 1, 3]
BG, BU, BS, BD, BW = 0, D, 2 * D, 2 * D + P, 3 * D + P
SU, SD, SS, SW = 0, D, 2 * D, 2 * D + 1

WQ, WK, WV, WO, WKI, WVI = range(6)
MATS = {0: 4, 2: 2, 3: 6}
BIAS = {(0, WQ): 0, (0, WK): 1, (0, WV): 2, (0, WO): 3, (2, WK): 4, (2, WV): 5,
        (3, WQ): 6, (3, WK): 7, (3, WV): 8, (3, WO): 9, (3, WKI): 10, (3, WVI): 11}
NB = len(BIAS) // 2
R3_KI, R3_K, R3_Q, R3_MIX = range(4)
ACC_DONE = {2: 2 * T, 3: 3 * T}


UNITS_OF_BATCH = 2 * NH
PARTS = 2 * G


def stage_steps(s, peak):
    a, r, d = s < B, peak and 1 <= s <= B, s >= 2
    plan = [(a, ("kv", s, 0)), (a, ("xt", s)), (r, ("neg", s - 1)), (a, ("kv", s, 1)), (a, ("kn", s, 0)),
            (r, ("re", s - 1, 0)), (a, ("st", s, 0)), (d, ("dt", s - 2, 0)), (r, ("re", s - 1, 1)),
            (a, ("tk", s, 0)), (d, ("dt", s - 2, 1)), (a, ("kn", s, 1)), (a, ("st", s, 1)), (a, ("q", s)),
            (a, ("kn", s, 4)), (a, ("kn", s, 5)), (a, ("tk", s, 1)), (a, ("st", s, 4)), (a, ("st", s, 5)),
            (a, ("kv", s, 2)), (a, ("tq", s, 0)), (a, ("kn", s, 2)), (d, ("ot", s - 2)), (a, ("st", s, 2)),
            (a, ("tq", s, 1)), (a, ("kv", s, 3)), (a, ("tk", s, 2)), (d, ("wo", s - 2)), (a, ("kn", s, 3)),
            (a, ("st", s, 3)), (s + 1 < B, ("ln", s + 1)), (a, ("tk", s, 3)),
            (s == B, ("early",))]
    return [st for there, st in plan if there]


COST = {"kv": 2.0, "xt": 0.8, "neg": 0.5, "re": 1.8, "kn": 0.3, "st": 0.6, "tk": 1.7, "q": 1.5, "dt": 1.0,
        "ot": 0.8, "tq": 1.8, "ln": 0.8, "wo": 1.2, "mx": 1.25, "early": 4.0}


def head_steps(c, lag):
    steps = []
    for u in range(UNITS_OF_BATCH):
        steps.append(("sc", c, u))
        part = u // 4 - lag
        if u % 4 == 2 and part >= 0:
            steps.append(("wg", c, part))
        if u % 4 == 3 and part >= 0 and part % 2:
            steps.append(("ev", c, part // 2))
    for part in range(PARTS - lag, PARTS):
        steps.append(("wg", c, part))
        if part % 2:
            steps.append(("ev", c, part // 2))
    return steps


def order(peak):
    steps = [("ln", 0)]
    for s in range(B + 2):
        stage = stage_steps(s, peak)
        if peak and s < B:
            stage += [("mx", s, h) for h in range(NH)]
        heads = head_steps(s - 1, 1 if peak else 2) if 0 <= s - 1 < B else []
        lead = 0
        if heads:
            lead = stage.index(("re", s - 1, QT - 1)) + 1 if peak else 0
        steps += stage[:lead]
        whole = sum(COST[st[0]] for st in stage[lead:])
        so_far, n = 0.0, 0
        for st in stage[lead:]:
            steps.append(st)
            so_far += COST[st[0]]
            upto = min(len(heads), int(len(heads) * so_far / whole))
            steps += heads[n:upto]
            n = upto
        steps += heads[n:]
    return steps


def uses(st):
    return [("k" if st[0] == "tk" else st[0], st[1], st[2], h) for h in range(2)]


def rings(blk, peak):
    turn, exchange = {}, {}
    for st in order(peak):
        if st[0] in ("tk", "tq", "re"):
            for n, u in enumerate(uses(st)):
                ring = exchange if n % 2 else turn
                ring[u] = len(ring)
        elif st[0] == "dt":
            for part in range(2 if blk == 3 else 1):
                exchange[("dt", st[1], st[2], part)] = len(exchange)
        elif st[0] in ("xt", "ot", "wo"):
            exchange[st] = len(exchange)
    return turn, exchange


PROJ = {0: 0, 1: 1, 4: 2, 5: 3, 2: 4, 3: 5}
PROJ_USE = {0: 0, 1: 1, 4: 2, 5: 2, 2: 3, 3: 4}
PROJ_BANKS = (5, 2, 3)


def flamingo(nc, a, out):
    first = -(-nc.sbuf_base // 64) * 64
    top = [0]

    def at(name, offset, shape, dt=F32):
        return nc.alloc_sbuf_tensor_at(name, shape, dt, offset=first + offset)

    def size(shape, dt=F32):
        return int(np.prod(shape[1:])) * (1 if dt == U8 else 4)

    def sb(name, shape, dt=F32):
        offset = top[0]
        top[0] += -(-size(shape, dt) // 32) * 32
        assert first + top[0] <= nc.sbuf_usable_end, name
        return at(name, offset, shape, dt)

    def region(nbytes):
        offset = top[0]
        top[0] += nbytes
        return offset

    x = sb("x", [P, T, D])
    ctx_hi = sb("ctx_hi", [P, KC, B * M], F32R)
    ctx_lo = sb("ctx_lo", [P, KC, B * M], F32R)

    KREG = region(32768)
    kst = [at(f"keys{i}", KREG + i * 16384, [P, NP, M], F32R) for i in range(2)]
    ff_xn = at("ff_xn", KREG, [P, T, D])
    ff_xh = at("ff_xh", KREG + 8192, [P, KC, B * S], F32R)
    ff_xl = at("ff_xl", KREG + 16384, [P, KC, B * S], F32R)
    cn_raw = at("cn_raw", KREG + 24576, [P, 2, KT, D])
    mask_u8 = at("mask_u8", KREG, [P, B, M], U8)
    mask_row = at("mask_row", KREG + 2048, [P, M], F32R)

    QREG = region(32768)
    qst = [at(f"queries{i}", QREG + i * 16384, [P, 2, NP, S], F32R) for i in range(2)]
    ff_s = at("ff_s", QREG, [P, 2, HALF])
    ff_h = at("ff_h", QREG + 4096, [P, 2, HALF])
    ff_hh = at("ff_hh", QREG + 8192, [P, 2, HALF], F32R)
    ff_hl = at("ff_hl", QREG + 12288, [P, 2, HALF], F32R)
    cn_hi = at("cn_hi", QREG, [P, 2, KT, D], F32R)
    cn_lo = at("cn_lo", QREG + 8192, [P, 2, KT, D], F32R)

    VS = NH * VW + 16
    values = sb("values", [P, 2, 5, VS])

    PREG = region(24576)
    probs = at("probs", PREG, [P, 3, 4, 2 * S])
    ff_raw = at("ff_raw", PREG, [P, 2, BW])
    ff_wh = at("ff_wh", PREG + 2 * BW * 4, [P, 2, BW], F32R)
    ff_wl = at("ff_wl", PREG + 4 * BW * 4, [P, 2, 3 * D], F32R)
    pn = at("pn", KREG + 8192, [P, 2, M])
    pt_hi = at("pt_hi", KREG + 12288, [P, 2, KT, P], F32R)
    pt_lo = at("pt_lo", KREG + 16384, [P, 2, KT, P], F32R)
    ct_raw = at("ct_raw", PREG, [P, B, KC, M])
    bias_raw = at("bias_raw", PREG + 16384, [P, NB, D])

    w_hi = sb("w_hi", [P, 6, KC, D], F32R)
    WL = region(12288)
    w_lo = at("w_lo", WL, [P, 6, KC, D], F32R)
    w_raw = at("w_raw", WL, [P, 6, KC, D])
    w2_nat = at("w2_nat", WL + 4 * 2048, [P, 2, KC, D])
    w2_spread = at("w2_spread", WL, [P, 2, D])

    SREG = region(12288)
    stk = at("stack_k", SREG, [P, NH, 64], F32R)
    stq = at("stack_q", SREG + 4096, [P, 2, NH, 64], F32R)
    combine_t = at("combine_t", SREG, [P, B * S], F32R)
    rt = SREG + 4096
    rt_l = at("rt_l", rt, [P, T, 16])
    rt_w = at("rt_w", rt + 512, [P, T, 24])
    rt_o = at("rt_o", rt + 1280, [P, T, 24])
    rt_8 = at("rt_8", rt + 2048, [P, T, 8])
    rt_s = at("rt_s", rt + 2304, [P, 4, T])
    rt_c = at("rt_c", rt + 2432, [P, T, 18])
    gate_raw = at("gate_raw", rt + 3008, [P, KC, 16])
    gate_hi = at("gate_hi", rt + 3136, [P, KC, 16], F32R)
    gate_lo = at("gate_lo", rt + 3264, [P, KC, 16], F32R)

    o_t = sb("o_t", [P, G, 2 * S])
    kn = sb("kn", [P, 2, D])
    bias = sb("bias", [P, NB, D], F32R)
    rows = sb("rows", [P, 4, D])
    xn = sb("xn", [P, QT, D])
    xt_hi = sb("xt_hi", [P, KC, S], F32R)
    xt_lo = sb("xt_lo", [P, KC, S], F32R)
    o_n = sb("o_n", [P, QT, D])
    ot_hi, ot_lo = xt_hi, xt_lo
    o_tmp = sb("o_tmp", [P, D])
    consts = sb("consts", [P, 12])
    is_img, text_at, not_img = (consts[:, 4 * i:4 * i + 4] for i in range(3))
    ones = sb("ones", [P, 2 * P], F32R)
    zeros = ones[:, P:2 * P]
    ident_r = sb("ident_r", [P, P], F32R)
    ident = ident_r[:, :].bitcast(F32)
    ident_raw = at("ident_raw", KREG, [P, P])
    w2_diag = at("w2_diag", KREG + 4096, [P, 4, P])
    negmax = sb("negmax", [P, 2, QT, NH, 2])
    g_all = sb("g_all", [P, 8])
    stat = sb("stat", [P, 8, 6])
    mv = sb("mv", [P, T, 2])
    ve = sb("ve", [P, T])
    rstd = sb("rstd", [P, T])
    half_neg = sb("half_neg", [P, T])
    rms = sb("rms", [P, 3, 6])
    small = sb("small", [P, 64])
    aug0 = sb("aug0", [P, B * KT])
    aug3 = sb("aug3", [P, KT, 5])
    keep3 = sb("keep3", [P, KT])
    mask_i = sb("mask_i", [P, B * KT], I32)
    lens_i = sb("lens_i", [P, 1], I32)
    fscale = sb("fscale", [P, 2])
    scal = sb("scal", [P, 3])
    res_scale = scal[:, 0:1]

    psum_cm = nc.psum_tensor("psum", [P, 8, 512], F32)
    ctx = ExitStack()
    psum = ctx.enter_context(psum_cm)

    sems = {}

    def sem(name):
        if name not in sems:
            sems[name] = ctx.enter_context(nc.semaphore(name))
        return sems[name]

    def attention_events(kind, blk):
        peak = blk != 0
        turn, exchange = rings(blk, peak)
        return {"xn_done": B, "b_full": len(exchange), "b_done": len(exchange), "b_hi": 0 if blk == 2 else 2 * B,
                "pj_full": 5 * B, "kq_hi": 6 * B, "kq_st": 6 * B, "v_done": KT * B,
                "t_full": len(turn), "t_act": len(turn),
                "st_full": UNITS_OF_BATCH * B, "p_exp": UNITS_OF_BATCH * B, "p_done": 0 if peak else PARTS * B,
                "mx_full": QT * NH * B if peak else 0, "mx_done": QT * NH * B if peak else 0,
                "neg_done": B if peak else 0, "o_full": PARTS * B, "o_done": G * B,
                "on_done": QT * B if peak else 0, "ss_done": 6 * B if blk == 3 else 0,
                "kn_done": {0: 0, 2: 2 * B, 3: 6 * B}[blk],
                "pw": {0: 2 * B, 2: B, 3: 7 * B}[blk]}[kind]

    counted = {}

    def before_attention(kind, blk):
        if (kind, blk) not in counted:
            counted[kind, blk] = sum(attention_events(kind, g) for g in (0, 2, 3) if g < blk)
        return counted[kind, blk]

    ATTENTION_EVENTS = (
        "xn_done b_full b_hi b_done pj_full kq_hi kq_st ss_done kn_done v_done t_full t_act "
        "st_full p_exp p_done mx_full mx_done o_full o_done neg_done on_done pw_in pw_out").split()
    FF_EVENTS = (
        "f_xn f_xt f_hi f_lo f_rt f_cb f_ct f_cth f_ctd f_pin f_pout f_gf f_sd f_uf f_td f_cf f_hm f_hh "
        "f_hr f_dd f_w1h f_w1r f_w2h f_w2r f_acc f_gh f_gl f_re f_ree").split()
    MEMORY_EVENTS = ("c_xn c_xt c_hi c_lo c_cnh c_cnl c_sf c_mx c_pn c_tf c_th c_tl c_pv c_x c_pin c_pout "
                     "c_mr q_int q_t q_tc q_diag q_sp").split()
    LOADS = ([f"d_x{b}" for b in range(B)] + [f"d_ct{b}" for b in range(B)] + [f"d_w0{m}" for m in range(4)] +
             [f"d_w3{m}" for m in range(6)] +
             ("d_small d_ident d_bias d_w2 d_w2n d_rows0 d_rows2 d_rows3 d_rows3a d_gate d_mask1 d_down d_ff0 d_ff1 "
              "d_cn0 d_cn1 d_out").split())
    START = ("v_init ct_l0 ones_done beta_used bp_used z_done g_tanh ct_h ct_l w0_h w0_l bias_h bias_l w2_l "
             "w3_l aug_done q_zeroed").split()
    CHAINS = ["dve", "pool"]
    for name in ATTENTION_EVENTS + FF_EVENTS + MEMORY_EVENTS + LOADS + START + CHAINS:
        sem(name)

    chain = {"dve": 0, "pool": 0}

    def wait(eng, kind, n):
        if isinstance(n, int) and n <= 0:
            return
        eng.wait_ge(sems[kind], n)

    def link(eng, name, ins):
        chain[name] += 1
        ins.then_inc(sems[name], 1)
        eng.wait_ge(sems[name], chain[name])

    def then(ins, kind):
        ins.then_inc(sems[kind], 1)

    def passes(eng, dst, lhs, rhs, start=True, stop=True, groups=KC):
        pairs = [(i, j) for i in range(len(lhs)) for j in range(len(rhs)) if i + j < 2]
        n = 0
        for k in range(groups):
            for i, j in pairs:
                last = eng.matmul(dst, lhs[i](k), rhs[j](k), start=start and n == 0,
                                  stop=stop and n == groups * len(pairs) - 1, skip_group_check=True)
                n += 1
        return last

    def attention(blk):
        peak = blk != 0
        steps = order(peak)
        turn, exchange = rings(blk, peak)
        hi_steps = [e for e in sorted(exchange, key=exchange.get)
                    if e[0] == "xt" or e[0] == "ot"]
        two = blk == 3

        def w(eng, kind, n):
            if n > 0:
                eng.wait_ge(sems[kind], n + before_attention("pw" if kind[:2] == "pw" else kind, blk))

        def proj(b, i):
            return 6 * b + PROJ[i]

        def through_kn(i):
            return blk == 3 or (blk == 2 and i >= 4)

        def place(b, i):
            bank = PROJ_BANKS[(5 * b + PROJ_USE[i]) % 3]
            half = D if i == 5 else 0
            return psum[:, bank, half:half + D]

        def full(b, i):
            return 5 * b + PROJ_USE[i] + 1

        def wait_proj_free(eng, b, i):
            if peak and b:
                w(eng, "mx_done", QT * NH * b)
            use = 5 * b + PROJ_USE[i] - 3
            if use < 0:
                return
            pb, pu = divmod(use, 5)
            pi = max(key for key, v in PROJ_USE.items() if v == pu)
            if blk == 3:
                w(eng, "kn_done", proj(pb, pi) + 1)
            elif through_kn(pi):
                w(eng, "kn_done", 2 * pb + 2)
            else:
                w(eng, "kq_st", proj(pb, pi) + 1)

        def kn_count(b, i):
            return proj(b, i) + 1 if blk == 3 else 2 * b + (i - 4) + 1

        def parts(mat):
            p = [lambda c: w_hi[:, mat, c, :], lambda c: w_lo[:, mat, c, :]]
            return p[:1] if blk == 2 and mat in (WQ, WO) else p

        def add_bias(eng, dst, mat, m=P, stop=True):
            i = BIAS[(blk, mat)]
            s = i // NB * 64
            return eng.matmul(dst, ones[s:s + 64, 0:m], bias[s:s + 64, i % NB, :], start=False,
                              stop=stop, skip_group_check=True)

        def xslice(hi, lo, q):
            return [lambda c: hi[:, c, q * P:(q + 1) * P], lambda c: lo[:, c, q * P:(q + 1) * P]]

        def ctx_cols(b, lo_, hi_):
            return [lambda c: ctx_hi[:, c, b * M + lo_:b * M + hi_],
                    lambda c: ctx_lo[:, c, b * M + lo_:b * M + hi_]]

        def src_of(b, i):
            n = proj(b, i)
            return kn[:, n % 2, :] if through_kn(i) else place(b, i)

        def stack_of(i):
            return stk[:, :, :] if i < 4 else stq[:, i - 4]

        def put_turned(eng, copy, u, src, kind):
            pairs, cols = slice(4 * u[3], 4 * u[3] + 4), slice(u[2] * P, (u[2] + 1) * P)
            src = src.rearrange("p (j c) -> p j c", c=P)
            if u[0] == "k":
                ins = copy(eng, kst[u[1] % 2][:, pairs, cols], src)
            else:
                for half in range(2):
                    rows_ = slice(64 * half, 64 * half + 64)
                    ins = copy(eng, qst[u[1] % 2][rows_, half, pairs, cols], src[rows_])
            then(ins, kind)

        def pe(eng, early):
            def project(mats, dst, mm_lhs):
                for mat, m in mats:
                    last = passes(eng, dst[0:m], mm_lhs(m), parts(mat), stop=False)
                    if (blk, mat) in BIAS:
                        last = add_bias(eng, dst[0:m], mat, m)
                return last

            def kv(b, kt):
                if b == 0 and kt == 0:
                    if blk == 0:
                        eng.wait_ge(sems["w0_l"], 1)
                        eng.wait_ge(sems["bias_l"], 1)
                    elif blk == 2:
                        eng.wait_ge(sems["w2_l"], 2)
                    else:
                        eng.wait_ge(sems["w3_l"], 6)
                if blk == 0 and kt == 0:
                    eng.wait_ge(sems["ct_l" if b else "ct_l0"], max(b, 1))
                wait_proj_free(eng, b, kt)
                mats = {WK: [(WK, P)], WV: [(WV, P)]}
                if two:
                    for m_, mi in ((WK, WKI), (WV, WVI)):
                        mats[m_] = [[(mi, P)], [(mi, P)], [(m_, P), (mi, 1)], [(m_, P)]][kt]
                lhs = lambda m: ctx_cols(b, kt * P, kt * P + m)
                dst = place(b, kt)
                project(mats[WK], dst, lhs)
                if blk == 0 and b == 0 and kt == 0:
                    eng.wait_ge(sems["w0_l"], 2)
                bank = PROJ_BANKS[(5 * b + PROJ_USE[kt]) % 3]
                then(project(mats[WV], psum[:, bank, D:2 * D], lhs), "pj_full")

            def xt(st):
                b = st[1]
                w(eng, "xn_done", b + 1)
                w(eng, "b_done", exchange[st])
                for c in range(KC):
                    for qt in range(QT):
                        last = eng.transpose(psum[:, 7, c * S + qt * P:c * S + (qt + 1) * P],
                                             xn[:, qt, c * P:(c + 1) * P], ident)
                then(last, "b_full")

            def q(b):
                if blk == 0 and b == 0:
                    eng.wait_ge(sems["w0_l"], 3)
                if blk == 2 and b == 0:
                    eng.wait_ge(sems["q_tc"], 2)
                w(eng, "b_done", exchange[("xt", b)] + 1)
                wait_proj_free(eng, b, 4)
                for qt in range(QT):
                    lhs = xslice(xt_hi, xt_lo, qt)
                    if blk == 2:
                        lhs = lhs[:1]
                    last = project([(WQ, P)], place(b, 4 + qt), lambda m: lhs)
                then(last, "pj_full")

            def turn_stacks(st):
                if st[0] == "tk":
                    w(eng, "kq_st", proj(st[1], st[2]) + 1)
                elif st[0] == "tq":
                    w(eng, "kq_st", proj(st[1], 5) + 1)
                else:
                    w(eng, "neg_done", st[1] + 1)
                for n, use in enumerate(uses(st)):
                    _, _, i, h = use
                    bank = 6 + n % 2
                    if n % 2:
                        w(eng, "b_done", exchange[use])
                    else:
                        w(eng, "t_act", turn[use])
                    src = (stk[:, :, :] if use[0] == "k" else stq[:, i]).rearrange(
                        "p (j two) c -> p j (two c)", two=2)
                    for j in range(4):
                        last = eng.matmul(psum[:, bank, j * P:(j + 1) * P], src[:, 4 * h + j, :], ident_r[:, :],
                                          start=True, stop=True, skip_group_check=True)
                    then(last, "b_full" if n % 2 else "t_full")

            def dt(b, qt):
                w(eng, "o_done", G * (b + 1))
                for part in range(2 if two else 1):
                    w(eng, "b_done", exchange[("dt", b, qt, part)])
                    for g in range(G):
                        last = eng.transpose(psum[:, 7, g * P:(g + 1) * P],
                                             o_t[:, g, part * S + qt * P:part * S + (qt + 1) * P], ident)
                    then(last, "b_full")

            def ot(st):
                w(eng, "b_done", exchange[st])
                if peak:
                    w(eng, "on_done", QT * (st[1] + 1))
                for c in range(KC):
                    for qt in range(QT):
                        last = eng.transpose(psum[:, 7, c * S + qt * P:c * S + (qt + 1) * P],
                                             o_n[:, qt, c * P:(c + 1) * P], ident)
                then(last, "b_full")

            def wo(st):
                if blk == 0 and st[1] == 0:
                    eng.wait_ge(sems["w0_l"], 4)
                    eng.wait_ge(sems["bias_l"], 3)
                w(eng, "b_done", exchange[st])
                for qt in range(QT):
                    lhs = xslice(ot_hi, ot_lo, qt)
                    dst = psum[:, 7, qt * S:(qt + 1) * S]
                    last = passes(eng, dst, lhs[:1] if blk == 2 else lhs, parts(WO),
                                  stop=blk == 2)
                    if blk != 2:
                        last = add_bias(eng, dst, WO)
                then(last, "b_full")

            def wait_turned(kind, b, h):
                if b == 0:
                    eng.wait_ge(sems["q_zeroed"], (0, 2, 3).index(blk) + 1)
                for ring, done, half in ((turn, "t_act", 0), (exchange, "b_done", 1)):
                    if half == h // (NH // 2):
                        last = max(ring[(kind, b, QT - 1, half)], ring[("k", b, KT - 1, half)])
                        w(eng, done, last + 1)

            def scores(c, u):
                n = UNITS_OF_BATCH * c + u
                if u in (0, UNITS_OF_BATCH // 2):
                    wait_turned("re" if peak else "tq", c, u // 2)
                w(eng, "p_exp", n - 1)
                part, j = divmod(u, 4)
                h = 4 * (part // 2) + j
                for i in range(2):
                    kt = 2 * (part % 2) + i
                    last = eng.matmul(psum[:, n % 2, i * S:(i + 1) * S],
                                      kst[c % 2][:, h // 2, kt * P:(kt + 1) * P],
                                      qst[c % 2][:, h % 2, h // 2, :], start=True, stop=True,
                                      skip_group_check=True)
                then(last, "st_full")

            def maxima(b, h):
                if h == 0:
                    w(eng, "kn_done" if blk == 3 else "kq_st", 6 * (b + 1))
                if h in (0, NH // 2):
                    wait_turned("tq", b, h)
                for qt in range(QT):
                    n = QT * (NH * b + h) + qt
                    w(eng, "mx_done", n - 2)
                    last = eng.matmul(psum[:, PROJ_BANKS[n % 3], :],
                                      qst[b % 2][:, h % 2, h // 2, qt * P:(qt + 1) * P],
                                      kst[b % 2][:, h // 2, :], start=True, stop=True)
                    then(last, "mx_full")

            def weigh(c, part):
                g, half = divmod(part, 2)
                n = PARTS * c + part
                if half == 0:
                    w(eng, "o_done", G * c + g)
                if peak:
                    w(eng, "p_exp", 4 * (n + 1))
                else:
                    w(eng, "p_done", n + 1)
                if half == 0:
                    plan = [(0, 0, 0, True), (1, 1, 0, False)]
                elif two:
                    plan = [(2, 0, 0, False), (4, 0, S, False), (3, 1, S, False)]
                else:
                    plan = [(2, 0, 0, False), (3, 1, 0, False)]
                for at_, (slot, kt, col, first_) in enumerate(plan):
                    for j in range(4):
                        h = 4 * g + j
                        last = eng.matmul(psum[32 * j:32 * j + 32, 4, col:col + S],
                                          values[:, c % 2, slot, h * VW:h * VW + 32],
                                          probs[:, n % 3, j, kt * S:(kt + 1) * S],
                                          start=first_, stop=half == 1 and at_ == len(plan) - 1,
                                          tile_position=(0, 32 * j), skip_group_check=True)
                then(last, "o_full")

            if blk:
                wait(eng, "f_acc", ACC_DONE[blk])
            for st in steps:
                if st[0] == "kv":
                    kv(st[1], st[2])
                elif st[0] == "xt":
                    xt(st)
                elif st[0] == "q":
                    q(st[1])
                elif st[0] in ("tk", "tq", "re"):
                    turn_stacks(st)
                elif st[0] == "dt":
                    dt(st[1], st[2])
                    if st[1:] == (B - 1, QT - 1):
                        early(eng)
                elif st[0] == "ot":
                    ot(st)
                elif st[0] == "wo":
                    wo(st)
                elif st[0] == "sc":
                    scores(st[1], st[2])
                elif st[0] == "mx":
                    maxima(st[1], st[2])
                elif st[0] == "wg":
                    weigh(st[1], st[2])

        def act(eng):
            if two:
                for buf in range(2):
                    eng.activation(values[:, buf, 2, 0:NH * VW].rearrange("p (h c) -> p h c", c=VW)[:, :, HD],
                                   is_img[:, 2:3].to_broadcast([P, NH]), ACT.Copy)

            def square(b, i):
                n = proj(b, i)
                w(eng, "kq_st", n - 1)
                w(eng, "pj_full", full(b, i))
                ins = eng.activation(kn[:, n % 2, :], place(b, i), ACT.Square,
                                     accum_out=rms[:, 0, n % 6:n % 6 + 1])
                then(ins, "ss_done")

            def kv(b, kt):
                if two:
                    square(b, kt)
                w(eng, "pj_full", full(b, kt))
                bank = PROJ_BANKS[(5 * b + PROJ_USE[kt]) % 3]
                src = psum[:, bank, D:2 * D].rearrange("p (h c) -> p h c", c=HD)

                def put(slot, scale=1.0):
                    dst = values[:, b % 2, slot, 0:NH * VW].rearrange("p (h c) -> p h c", c=VW)
                    return eng.activation(dst[:, :, 0:HD], src, ACT.Copy, scale=scale)

                if two and kt == 2:
                    put(2, is_img[:, 2:3])
                    then(put(4, not_img[:, 2:3]), "v_done")
                else:
                    then(put(kt), "v_done")

            def stack(b, i):
                n = proj(b, i)
                if through_kn(i):
                    w(eng, "kn_done", kn_count(b, i))
                else:
                    w(eng, "pj_full", full(b, i))
                if i < 4:
                    if 4 * b + i:
                        pb, pi = divmod(4 * b + i - 1, 4)
                        w(eng, "b_full", exchange[("k", pb, pi, 1)] + 1)
                    places = slice(0, 3, 2)
                else:
                    if b:
                        w(eng, "b_full", exchange[("re" if peak else "tq", b - 1, i - 4, 1)] + 1)
                    places = slice(0, 2)
                dst = stack_of(i).rearrange("p h (s c) -> p h s c", c=HD)[:, :, places, :]
                src = src_of(b, i).rearrange("p (h one c) -> p h one c", one=1, c=HD)
                then(eng.activation(dst, src.to_broadcast([P, NH, 2, HD]), ACT.Copy), "kq_hi")

            def exponentials(c, u):
                n = UNITS_OF_BATCH * c + u
                w(eng, "st_full", n + 1)
                if blk == 0 and n == 0:
                    eng.wait_ge(sems["ct_l"], B - 1)
                if u % 4 == 0:
                    w(eng, "o_full", n // 4 - 2)
                then(eng.activation(probs[:, n // 4 % 3, u % 4, :], psum[:, n % 2, :], ACT.Exp, scale=SCALE),
                     "p_exp")

            def evacuate(c, g):
                w(eng, "o_full", PARTS * c + 2 * (g + 1))
                if g == 0:
                    w(eng, "b_full", exchange[("dt", c - 1, QT - 1, int(two))] + 1 if c else 0)
                wd = 2 * S if two else S
                then(eng.activation(o_t[:, g, 0:wd], psum[:, 4, 0:wd], ACT.Copy), "o_done")

            for st in steps:
                if st[0] == "kv":
                    kv(st[1], st[2])
                elif st[0] == "q" and two:
                    for qt in range(QT):
                        square(st[1], 4 + qt)
                elif st[0] == "st":
                    stack(st[1], st[2])
                elif st[0] in ("tk", "tq", "re"):
                    for use in uses(st)[::2]:
                        w(eng, "t_full", turn[use] + 1)
                        put_turned(eng, lambda e, dst, src: e.activation(dst, src, ACT.Copy), use,
                                   psum[:, 6, :], "t_act")
                elif st in hi_steps and blk != 2:
                    w(eng, "b_full", exchange[st] + 1)
                    dst = xt_hi if st[0] == "xt" else ot_hi
                    then(eng.activation(dst[:, :, :].rearrange("p c t -> p (c t)"), psum[:, 7, :],
                                        ACT.Copy), "b_hi")
                elif st[0] == "sc":
                    exponentials(st[1], st[2])
                elif st[0] == "ev":
                    evacuate(st[1], st[2])

        def pool_root(eng, n, src, dst, width, times=None):
            w(eng, "pw_in", n + 1)
            ins = eng.tensor_tensor(dst, src, half_neg[:, 0:width], ALU.pow)
            if times is not None:
                link(eng, "pool", ins)
                ins = eng.tensor_tensor(dst, dst, times, ALU.mult)
            then(ins, "pw_out")

        def pool(eng, early, between=None):
            n = 0
            for st in steps:
                if st == ("xt", 0) and between:
                    between()
                    eng.wait_ge(sems["ct_l"], B - 1)
                if st == ("xt", 0):
                    w(eng, "pw_out", n)
                    for half in range(2):
                        for buf in range(2):
                            r = 64 * (1 - half)
                            ins = eng.memset(qst[buf][r:r + 64, half].bitcast(F32), 0.0)
                        if half == 0:
                            link(eng, "pool", ins)
                    then(ins, "q_zeroed")
                    eng.wait_ge(sems["q_zeroed"], (0, 2, 3).index(blk) + 1)
                if st[0] == "early":
                    early(eng)
                elif st[0] == "ln":
                    pool_root(eng, n, ve[:, 0:QT], rstd[:, 0:QT], QT)
                    n += 1
                elif two and st[0] == "kv":
                    i = PROJ[st[2]]
                    pool_root(eng, n, rms[:, 1, i:i + 1], rms[:, 2, i:i + 1], 1, keep3[:, st[2]:st[2] + 1])
                    n += 1
                elif two and st[0] == "q":
                    for qt in range(QT):
                        i = PROJ[4 + qt]
                        pool_root(eng, n, rms[:, 1, i:i + 1], rms[:, 2, i:i + 1], 1)
                        n += 1
                elif blk == 0 and st[0] == "wo":
                    pool_root(eng, n, ve[:, 2:2 + QT], rstd[:, 2:2 + QT], QT)
                    n += 1

        def dve(eng, early, between={}):
            roots = [0]
            root_of = {}

            def dl(ins):
                link(eng, "dve", ins)

            def ask_root(ins, key):
                then(ins, "pw_in")
                root_of[key] = roots[0]
                roots[0] += 1

            def quantize(src, qt, slot):
                sc = small[:, slot:slot + 1]
                inv = small[:, slot + 1:slot + 2]
                dl(eng.tensor_reduce(sc, src, AX.X, ALU.max, apply_absolute_value=True))
                dl(eng.tensor_scalar(sc, sc, 1.0 / 127.0, 1e-8, ALU.mult, ALU.max))
                dl(eng.reciprocal(inv, sc))
                dl(eng.tensor_scalar(src, src, inv, MAGIC, ALU.mult, ALU.add))
                return eng.tensor_scalar(src, src, -MAGIC, 127.0, ALU.add, ALU.min)

            def ln(b):
                if blk == 0 and b:
                    eng.wait_ge(sems[f"d_x{b}"], 16)
                if b:
                    w(eng, "b_full", exchange[("xt", b - 1)] + 1)
                for qt in range(QT):
                    last = eng.bn_stats(stat[:, qt, :], x[:, QT * b + qt, :])
                dl(last)
                for qt in range(QT):
                    last = eng.bn_aggr(mv[:, qt, :], stat[:, qt, :])
                dl(last)
                ask_root(eng.tensor_scalar(ve[:, 0:QT], mv[:, 0:QT, 1], LN_EPS, None, ALU.add), ("ln", b))
                w(eng, "pw_out", root_of[("ln", b)] + 1)
                for qt in range(QT):
                    ins = eng.tensor_scalar(xn[:, qt, :], x[:, QT * b + qt, :], mv[:, qt, 0:1],
                                            rstd[:, qt:qt + 1], ALU.subtract, ALU.mult)
                    if blk == 2:
                        dl(ins)
                        ins = quantize(xn[:, qt, :], qt, 16 * (b % 2) + 2 * qt)
                then(ins, "xn_done")

            def mean_square(n):
                w(eng, "ss_done", n + 1)
                ask_root(eng.tensor_scalar(rms[:, 1, n % 6:n % 6 + 1], rms[:, 0, n % 6:n % 6 + 1],
                                           1.0 / D, RMS_EPS, ALU.mult, ALU.add), n)

            def kn_step(b, i):
                n = proj(b, i)
                w(eng, "kq_hi", n - 1)
                dst = kn[:, n % 2, :]
                if two:
                    if i < 4:
                        w(eng, "v_done", 4 * b + i + 1)
                    else:
                        w(eng, "ss_done", proj(b, 5) + 1)
                    w(eng, "pw_out", root_of[n] + 1)
                    gain = {0: R3_KI, 1: R3_KI, 2: R3_MIX, 3: R3_K, 4: R3_Q, 5: R3_Q}[i]
                    ins = eng.scalar_tensor_tensor(dst, place(b, i), rms[:, 2, n % 6:n % 6 + 1],
                                                   rows[:, gain, :], ALU.mult, ALU.mult)
                else:
                    w(eng, "pj_full", full(b, i))
                    sc = 16 * (b % 2) + 2 * (i - 4)
                    dl(eng.scalar_tensor_tensor(dst, place(b, i), small[:, sc:sc + 1],
                                                w2_spread[:, 0, :], ALU.mult, ALU.mult))
                    ins = eng.tensor_tensor(dst, dst, rows[:, 0, :], ALU.add)
                then(ins, "kn_done")

            def stack(b, i):
                n = proj(b, i)
                w(eng, "kq_hi", n + 1)
                if not through_kn(i):
                    if i < 4:
                        w(eng, "v_done", 4 * b + i + 1)
                    else:
                        w(eng, "kq_hi", proj(b, 5) + 1)
                if through_kn(i):
                    w(eng, "kn_done", kn_count(b, i))
                st_ = stack_of(i)
                if i < 4 and blk != 2:
                    cols = aug3[:, i, :] if two else aug0[:, KT * b + i:KT * b + i + 1]
                    wd = 5 if two else 1
                    at_ = 48 if two else 52
                    eng.tensor_copy(st_[:, :, at_:at_ + wd],
                                    cols.rearrange("p (one c) -> p one c", one=1).to_broadcast([P, NH, wd]))
                if i >= 4 and peak:
                    eng.memset(st_[:, :, 48:52].bitcast(F32), 0.0)
                lane = st_.rearrange("p h (s c) -> p h s c", c=HD)
                at_lo = 1 if i < 4 else 2
                then(eng.tensor_tensor(lane[:, :, at_lo, :],
                                       src_of(b, i).rearrange("p (h c) -> p h c", c=HD),
                                       lane[:, :, 0, :].bitcast(F32), ALU.subtract), "kq_st")

            def neg(b):
                w(eng, "mx_done", QT * NH * (b + 1))
                wd = 2 if two else 1
                for part in range(2):
                    for qt in range(QT):
                        st_ = stq[:, qt, :, 48:52].rearrange("p h (a two) -> p h a two", two=2)
                        m = negmax[:, b % 2, qt, :, 0:wd]
                        dst = st_[:, :, 0:wd, part]
                        if part == 0:
                            ins = eng.tensor_copy(dst, m)
                        else:
                            ins = eng.tensor_tensor(dst, m, st_[:, :, 0:wd, 0].bitcast(F32), ALU.subtract)
                    if part == 0:
                        dl(ins)
                    else:
                        then(ins, "neg_done")

            def dt(b, qt):
                inv = small[:, 32:48]
                o = o_n[:, qt, :].rearrange("p (h c) -> p h c", c=HD)
                for part in range(2 if two else 1):
                    e = exchange[("dt", b, qt, part)]
                    w(eng, "b_full", e + 1)
                    got = psum[:, 7, :].rearrange("p (h c) -> p h c", c=32)
                    total = got[:, :, HD]
                    dl(eng.reciprocal(inv, total))
                    if blk == 0:
                        again = small[:, 48:64]
                        dl(eng.tensor_tensor(again, total, inv, ALU.mult))
                        dl(eng.tensor_scalar(again, again, 1e-8, None, ALU.add))
                        dl(eng.reciprocal(again, again))
                        dl(eng.tensor_tensor(inv, inv, again, ALU.mult))
                    dst = o if part == 0 else o_tmp[:, :].rearrange("p (h c) -> p h c", c=HD)
                    spread = inv.rearrange("p (h one) -> p h one", one=1).to_broadcast([P, NH, HD])
                    then(eng.tensor_tensor(dst, got[:, :, 0:HD], spread, ALU.mult), "b_done")
                    w(eng, "b_done", e + 1)
                if two:
                    then(eng.tensor_tensor(o_n[:, qt, :], o_n[:, qt, :], o_tmp[:, :], ALU.add), "on_done")
                elif blk == 2:
                    then(quantize(o_n[:, qt, :], qt, 4 + 16 * (b % 2) + 2 * qt), "on_done")

            def exchange_lo(st):
                e = exchange[st]
                hi, lo = (xt_hi, xt_lo) if st[0] == "xt" else (ot_hi, ot_lo)
                flat = lambda t: t[:, :, :].rearrange("p c t -> p (c t)")
                if blk == 2:
                    w(eng, "b_full", e + 1)
                    ins = eng.tensor_scalar(flat(hi), psum[:, 7, :], -127.0, None, ALU.max)
                else:
                    w(eng, "b_hi", hi_steps.index(st) + 1)
                    ins = eng.tensor_tensor(flat(lo), psum[:, 7, :], flat(hi).bitcast(F32), ALU.subtract)
                then(ins, "b_done")

            def wo(st):
                b, e = st[1], exchange[st]
                w(eng, "b_full", e + 1)
                tg = g_all[:, blk:blk + 1]
                if two:
                    for qt in range(QT):
                        xt_ = x[:, QT * b + qt, :]
                        ins = eng.scalar_tensor_tensor(xt_, psum[:, 7, qt * S:(qt + 1) * S], tg, xt_,
                                                       ALU.mult, ALU.add)
                    then(ins, "b_done")
                    w(eng, "b_done", e + 1)
                    return
                for qt in range(QT):
                    src = psum[:, 7, qt * S:(qt + 1) * S]
                    if blk == 0:
                        ins = eng.tensor_scalar(o_n[:, qt, :], src, res_scale, None, ALU.mult)
                    else:
                        sc = 4 + 16 * (b % 2) + 2 * qt
                        ins = eng.scalar_tensor_tensor(o_n[:, qt, :], src, small[:, sc:sc + 1],
                                                       w2_spread[:, 1, :], ALU.mult, ALU.mult)
                then(ins, "b_done")
                w(eng, "b_done", e + 1)
                if blk == 0:
                    eng.wait_ge(sems["d_rows0"], 32)
                    for qt in range(QT):
                        ins = eng.bn_stats(stat[:, 2 + qt, :], o_n[:, qt, :])
                    dl(ins)
                    for qt in range(QT):
                        ins = eng.bn_aggr(mv[:, 2 + qt, :], stat[:, 2 + qt, :])
                    dl(ins)
                    ask_root(eng.tensor_scalar(ve[:, 2:2 + QT], mv[:, 2:2 + QT, 1], LN_EPS, None, ALU.add),
                             ("wo", b))
                    w(eng, "pw_out", root_of[("wo", b)] + 1)
                    for qt in range(QT):
                        ins = eng.tensor_scalar(o_n[:, qt, :], o_n[:, qt, :], mv[:, 2 + qt, 0:1],
                                                rstd[:, 2 + qt:3 + qt], ALU.subtract, ALU.mult)
                    dl(ins)
                    for qt in range(QT):
                        ins = eng.tensor_tensor(o_n[:, qt, :], o_n[:, qt, :], rows[:, 0, :], ALU.mult)
                    dl(ins)
                for qt in range(QT):
                    ins = eng.tensor_tensor(o_n[:, qt, :], o_n[:, qt, :], rows[:, 1, :], ALU.add)
                used = "beta_used" if blk == 0 else "bp_used"
                then(ins, used)
                wait(eng, used, b + 1)
                for qt in range(QT):
                    xt_ = x[:, QT * b + qt, :]
                    ins = eng.scalar_tensor_tensor(xt_, o_n[:, qt, :], tg, xt_, ALU.mult, ALU.add)
                dl(ins)

            def clip(c, part):
                n = PARTS * c + part
                w(eng, "p_exp", 4 * (n + 1))
                pr = probs[:, n % 3, :, :].rearrange("p j c -> p (j c)")
                then(eng.tensor_scalar(pr, pr, EXP50N, EXP50P, ALU.max, ALU.min), "p_done")

            def maxima(b, h):
                for qt in range(QT):
                    n = QT * (NH * b + h) + qt
                    w(eng, "mx_full", n + 1)
                    bank = psum[:, PROJ_BANKS[n % 3], :]
                    dst = negmax[:, b % 2, qt, h, :]
                    if two:
                        eng.tensor_reduce(dst[:, 0:1], bank[:, 0:IMG], AX.X, ALU.max, negate=True)
                        ins = eng.tensor_reduce(dst[:, 1:2], bank[:, IMG:M], AX.X, ALU.max, negate=True)
                    else:
                        ins = eng.tensor_reduce(dst[:, 0:1], bank, AX.X, ALU.max, negate=True)
                    then(ins, "mx_done")

            def prepare():
                eng.memset(stk[:, :, 48:64].bitcast(F32), 0.0)
                dl(eng.memset(stq[:, :, :, 48:64].bitcast(F32), 0.0))
                if blk == 2:
                    eng.memset(stk[:, :, 48:50].bitcast(F32), 1.0)
                dl(eng.memset(stq[:, :, :, 52:53].bitcast(F32), 1.0))

            for st in steps:
                if st[0] == "ln":
                    ln(st[1])
                    if st[1] == 0:
                        prepare()
                elif st[0] == "early":
                    early(eng)
                elif st[0] == "kv" and two:
                    mean_square(proj(st[1], st[2]))
                elif st[0] == "q" and two:
                    for qt in range(QT):
                        mean_square(proj(st[1], 4 + qt))
                elif st[0] == "kn" and through_kn(st[2]):
                    kn_step(st[1], st[2])
                elif st[0] == "st":
                    stack(st[1], st[2])
                elif st[0] == "neg":
                    neg(st[1])
                elif st[0] in ("tk", "tq", "re"):
                    for use in uses(st)[1::2]:
                        w(eng, "b_full", exchange[use] + 1)
                        put_turned(eng, lambda e, dst, src: e.tensor_copy(dst, src), use, psum[:, 7, :],
                                   "b_done")
                elif st[0] in ("xt", "ot"):
                    exchange_lo(st)
                elif st[0] == "dt":
                    dt(st[1], st[2])
                elif st[0] == "wo":
                    wo(st)
                elif st[0] == "sc" and not peak and st[2] % 4 == 3:
                    clip(st[1], st[2] // 4)
                elif st[0] == "mx":
                    maxima(st[1], st[2])
                if st in between:
                    between[st]()

        return pe, act, pool, dve

    def counts(f, kind):
        n, t = 2 * TILES[f], TILES[f]
        if kind in ("f_gf", "f_hm", "f_hh", "f_hr", "f_dd"):
            return n
        if kind in ("f_w1h", "f_w2h"):
            return t
        if kind in ("f_xt", "f_hi", "f_lo"):
            return 4
        if kind in ("f_xn", "f_acc"):
            return T
        if kind in ("f_pin", "f_pout"):
            return 2
        if kind == "f_d0":
            return -(-t // 2)
        if kind == "f_d1":
            return t // 2
        if f == 2:
            return 0
        return {"f_sd": n, "f_uf": n, "f_td": n, "f_cf": n, "f_w1r": t, "f_w2r": t, "f_rt": 1, "f_re": 1,
                "f_ree": 1, "f_cb": 1, "f_ct": 2, "f_cth": 2, "f_ctd": 2, "f_gw": 1, "f_gh": 1, "f_gl": 1}[kind]

    def feed_forward(f):
        sign = f == 2
        tiles = TILES[f]
        N = 2 * tiles
        E = 0 if sign else FFN[f]["E"]
        K = 0 if sign else FFN[f]["K"]
        EL = E + 2 if f == 0 else E
        EC = E + 1

        def before(kind):
            return sum(counts(g, kind) for g in range(f))

        def w(eng, kind, n):
            if isinstance(n, int) and before(kind) + n <= 0:
                return
            eng.wait_ge(sems[kind], n + before(kind))

        def w_tile(eng, slot, j):
            eng.wait_ge(sems[f"d_ff{slot}"], (j + (before(f"f_d{slot}") + 1)) * 16)

        def over_tiles(eng, step):
            pairs = (tiles - 1) // 2
            with eng.Fori(0, pairs) as i:
                step(i * 2 + 1, 1, i)
                step(i * 2 + 2, 0, i + 1)
            if tiles % 2 == 0:
                step(tiles - 1, 1, tiles // 2 - 1)

        def acc(t):
            return psum[:, t // 2, t % 2 * D:(t % 2 + 1) * D]

        def wcols(base, c0, slot):
            return lambda c: base[:, slot, c0 + c * P:c0 + (c + 1) * P]

        def tokens(hf):
            return [lambda c: ff_xh[:, c, hf * HALF:(hf + 1) * HALF],
                    lambda c: ff_xl[:, c, hf * HALF:(hf + 1) * HALF]]

        FIRST = (0, 6, T)

        def turn_tokens(eng, hf):
            for c in range(KC):
                for t in range(4):
                    if c == 0:
                        w(eng, "f_xn", 4 * hf + t + 1)
                    last = eng.transpose(psum[:, 4 + 2 * hf + c, t * P:(t + 1) * P],
                                         ff_xn[:, 4 * hf + t, c * P:(c + 1) * P], ident)
                then(last, "f_xt")

        def roots(eng, i):
            w(eng, "f_pin", i + 1)
            tiles_ = slice(FIRST[i], FIRST[i + 1])
            then(eng.tensor_tensor(rstd[:, tiles_], ve[:, tiles_], half_neg[:, tiles_], ALU.pow), "f_pout")

        def normalize(eng, i):
            tiles_ = range(FIRST[i], FIRST[i + 1])
            for t in tiles_:
                last = eng.bn_stats(stat[:, t, :], x[:, t, :])
            link(eng, "dve", last)
            for t in tiles_:
                last = eng.bn_aggr(mv[:, t, :], stat[:, t, :])
            link(eng, "dve", last)
            cols = slice(FIRST[i], FIRST[i + 1])
            then(eng.tensor_scalar(ve[:, cols], mv[:, cols, 1], LN_EPS, None, ALU.add), "f_pin")
            w(eng, "f_pout", i + 1)
            for t in tiles_:
                then(eng.tensor_scalar(ff_xn[:, t, :], x[:, t, :], mv[:, t, 0:1], rstd[:, t:t + 1],
                                       ALU.subtract, ALU.mult), "f_xn")
            w(eng, "f_xn", FIRST[i + 1])

        early = (lambda eng: turn_tokens(eng, 0), lambda eng: roots(eng, 0), lambda eng: normalize(eng, 0))

        def pe(eng):
            def gate(n, slot, hf):
                w(eng, "f_hm" if sign else "f_sd", n - 1)
                lhs = [wcols(ff_wh, BG, slot)] + ([] if sign else [wcols(ff_wl, BG, slot)])
                then(passes(eng, psum[:, 4 + hf, :], lhs, tokens(hf)), "f_gf")

            def up(n, slot, hf):
                w(eng, "f_td", n)
                lhs = [wcols(ff_wh, BU, slot), wcols(ff_wl, BU, slot)]
                then(passes(eng, psum[:, 6, :], lhs, tokens(hf)), "f_uf")

            def spread(n, slot, hf):
                w(eng, "f_hm", n)
                then(eng.matmul(psum[:, 7, :], ff_wh[0:64, slot, BS:BS + P],
                                combine_t[0:64, hf * HALF:(hf + 1) * HALF], start=True, stop=True), "f_cf")

            def down(n, tile, slot, hf):
                w(eng, "f_hr", n + 1)
                if hf == 0:
                    w(eng, "f_w2h" if sign else "f_w2r", tile + 1)
                c0 = SD if sign else BD
                rhs = [lambda c: ff_wh[:, slot, c0:c0 + D]]
                if not sign:
                    rhs.append(lambda c: ff_wl[:, slot, 2 * D:3 * D])
                for t in range(4):
                    cols = slice(t * P, (t + 1) * P)
                    last = passes(eng, acc(4 * hf + t), [lambda c: ff_hh[:, hf, cols],
                                                         lambda c: ff_hl[:, hf, cols]],
                                  rhs, start=False, stop=False, groups=1)
                then(last, "f_dd")

            def clear_sums(banks):
                for bank in banks:
                    eng.matmul(psum[:, bank, :], zeros, ff_xh[:, 0, 0:HALF], start=True, stop=False,
                               skip_group_check=True)

            turn_tokens(eng, 1)
            w(eng, "f_lo", 4)
            if not sign:
                w(eng, "f_gl", 1)
                for t in range(T):
                    cols = slice(t * P, (t + 1) * P)
                    last = passes(eng, psum[:, 0, t * EL:(t + 1) * EL],
                                  [lambda c: ff_xh[:, c, cols], lambda c: ff_xl[:, c, cols]],
                                  [lambda c: gate_hi[:, c, 0:EL], lambda c: gate_lo[:, c, 0:EL]])
                then(last, "f_rt")
            w(eng, "f_w1h" if sign else "f_w1r", 1)
            gate(0, 0, 0)
            if not sign:
                up(0, 0, 0)
                gate(1, 0, 1)
                w(eng, "f_cb", 1)
                for t in range(T):
                    last = eng.transpose(psum[0:EC, 1 + t // 4, t % 4 * P:(t % 4 + 1) * P],
                                         rt_c[:, t, 0:EC], ident)
                    if t % 4 == 3:
                        then(last, "f_ct")
                clear_sums((0, 3))
                w(eng, "f_ctd", 2)
                spread(0, 0, 0)
                clear_sums((1, 2))
                up(1, 0, 1)
                spread(1, 0, 1)
            else:
                clear_sums(range(4))
                gate(1, 0, 1)

            def step(tile, slot, j):
                for hf in range(2):
                    n = tile * 2 + hf
                    if hf == 0:
                        w(eng, "f_w1h" if sign else "f_w1r", tile + 1)
                    gate(n, slot, hf)
                    down(n - 2, tile - 1, 1 - slot, hf)
                    if not sign:
                        up(n, slot, hf)
                        spread(n, slot, hf)

            over_tiles(eng, step)
            for hf in range(2):
                down(N - 2 + hf, tiles - 1, (tiles - 1) % 2, hf)

        def act(eng):
            def half_hi(n, hf):
                w(eng, "f_hm", n + 1)
                w(eng, "f_dd", n - 1)
                then(eng.activation(ff_hh[:, hf, :], ff_h[:, hf, :], ACT.Copy), "f_hh")

            def split_up(tile, slot, j):
                w_tile(eng, slot, j)
                if sign:
                    w(eng, "f_hm", tile * 2 - 2)
                    w(eng, "f_gf", tile * 2 - 2)
                    eng.activation(fscale[:, slot:slot + 1], ff_raw[:, slot, SS:SS + 1], ACT.Copy)
                    ins = eng.activation(ff_wh[:, slot, SU:SU + D], ff_raw[:, slot, SU:SU + D], ACT.Sign)
                else:
                    w(eng, "f_cf", tile * 2 - 2)
                    ins = eng.activation(ff_wh[:, slot, 0:BD], ff_raw[:, slot, 0:BD], ACT.Copy)
                then(ins, "f_w1h")

            def split_down(tile, slot):
                w(eng, "f_dd", tile * 2 - 2)
                c0 = SD if sign else BD
                then(eng.activation(ff_wh[:, slot, c0:c0 + D], ff_raw[:, slot, c0:c0 + D],
                                    ACT.Sign if sign else ACT.Copy), "f_w2h")

            def silu(n, hf):
                w(eng, "f_gf", n + 1)
                w(eng, "f_hm", n - 1)
                then(eng.activation(ff_s[:, hf, :], psum[:, 4 + hf, :], ACT.Silu), "f_sd")

            split_up(0, 0, 0)
            split_down(0, 0)
            for i in range(4):
                w(eng, "f_xt", i + 1)
                hf, c = divmod(i, 2)
                then(eng.activation(ff_xh[:, c, hf * HALF:(hf + 1) * HALF], psum[:, 4 + i, :], ACT.Copy),
                     "f_hi")
                if i == 1 and not sign:
                    eng.wait_ge(sems["d_gate"], 16 * (ROUTED.index(f) + 1))
                    then(eng.activation(gate_hi[:, :, :], gate_raw[:, :, :], ACT.Copy), "f_gh")
            if tiles > 1:
                split_up(1, 1, 0)
            if not sign:
                w(eng, "f_re", 1)
                if f == 0:
                    logits = psum[:, 0, 0:T * EL].rearrange("p (t e) -> p t e", e=EL)
                    eng.activation(rt_c[:, :, E], logits[:, :, E], ACT.Exp, scale=-1.0)
                then(eng.activation(rt_w[:, :, 0:E], rt_w[:, :, 0:E], ACT.Exp), "f_ree")
                silu(0, 0)
                silu(1, 1)
                for i in range(2):
                    w(eng, "f_ct", i + 1)
                    then(eng.activation(combine_t[0:EC, i * HALF:(i + 1) * HALF], psum[0:EC, 1 + i, :],
                                        ACT.Copy), "f_cth")
            half_hi(0, 0)
            split_down(1, 1)

            def step(tile, slot, j, more=True):
                for hf in range(2):
                    n = tile * 2 + hf
                    if not sign:
                        silu(n, hf)
                    if more and hf == 0:
                        split_up(tile + 1, 1 - slot, j + slot)
                    half_hi(n - 1, 1 - hf)
                    if more and hf == 1:
                        split_down(tile + 1, 1 - slot)

            pairs = (tiles - 1) // 2
            if tiles % 2 == 0:
                with eng.Fori(0, pairs) as i:
                    step(i * 2 + 1, 1, i)
                    step(i * 2 + 2, 0, i + 1)
                step(tiles - 1, 1, tiles // 2 - 1, more=False)
            else:
                with eng.Fori(0, pairs - 1) as i:
                    step(i * 2 + 1, 1, i)
                    step(i * 2 + 2, 0, i + 1)
                step(tiles - 2, 1, pairs - 1)
                step(tiles - 1, 0, pairs, more=False)
            half_hi(N - 1, 1)

        def pool(eng, extra=None):
            roots(eng, 1)
            if sign:
                if extra:
                    extra()
                return

            def lo(tile, slot):
                w(eng, "f_w1h", tile + 1)
                then(eng.tensor_tensor(ff_wl[:, slot, 0:2 * D], ff_raw[:, slot, 0:2 * D],
                                       ff_wh[:, slot, 0:2 * D].bitcast(F32), ALU.subtract), "f_w1r")
                w(eng, "f_w2h", tile + 1)
                then(eng.tensor_tensor(ff_wl[:, slot, 2 * D:3 * D], ff_raw[:, slot, BD:BD + D],
                                       ff_wh[:, slot, BD:BD + D].bitcast(F32), ALU.subtract), "f_w2r")

            lo(0, 0)
            if extra:
                extra()
            over_tiles(eng, lambda tile, slot, j: lo(tile, slot))

        def dve(eng):
            def dl(ins):
                link(eng, "dve", ins)

            normalize(eng, 1)
            if not sign:
                eng.memset(combine_t[0:64, :].bitcast(F32), 0.0)
                eng.memset(rt_w[:, :, E:24], -1.0)
                if f:
                    eng.memset(rt_c[:, :, E:E + 1], 1.0)
            for i in range(4):
                w(eng, "f_hi", i + 1)
                hf, c = divmod(i, 2)
                cols = slice(hf * HALF, (hf + 1) * HALF)
                then(eng.tensor_tensor(ff_xl[:, c, cols], psum[:, 4 + i, :], ff_xh[:, c, cols].bitcast(F32),
                                       ALU.subtract), "f_lo")
                if i == 1 and not sign:
                    w(eng, "f_gh", 1)
                    then(eng.tensor_tensor(gate_lo[:, :, :], gate_raw[:, :, :],
                                           gate_hi[:, :, :].bitcast(F32), ALU.subtract), "f_gl")

            def gated(n, hf):
                w(eng, "f_sd", n + 1)
                w(eng, "f_uf", n + 1)
                then(eng.tensor_tensor(ff_s[:, hf, :], ff_s[:, hf, :], psum[:, 6, :], ALU.mult), "f_td")

            def weighted(n, hf):
                w(eng, "f_cf", n + 1)
                w(eng, "f_td", n + 1)
                w(eng, "f_hh", n - 1)
                then(eng.tensor_tensor(ff_h[:, hf, :], ff_s[:, hf, :], psum[:, 7, :], ALU.mult), "f_hm")

            def relu(n, hf, tile, slot):
                w(eng, "f_gf", n + 1)
                if hf == 0:
                    w(eng, "f_w1h", tile + 1)
                w(eng, "f_hr", n - 1)
                then(eng.tensor_scalar(ff_h[:, hf, :], psum[:, 4 + hf, :], fscale[:, slot:slot + 1], 0.0,
                                       ALU.mult, ALU.max), "f_hm")

            def half_lo(n, hf):
                w(eng, "f_hh", n + 1)
                then(eng.tensor_tensor(ff_hl[:, hf, :], ff_h[:, hf, :], ff_hh[:, hf, :].bitcast(F32),
                                       ALU.subtract), "f_hr")

            def route():
                logits = psum[:, 0, 0:T * EL].rearrange("p (t e) -> p t e", e=EL)[:, :, 0:E]
                spread = lambda i: rt_s[:, i, :].rearrange("p (t one) -> p t one", one=1).to_broadcast([P, T, E])
                p_ = rt_w[:, :, 0:E]
                w(eng, "f_rt", 1)
                dl(eng.tensor_reduce(rt_s[:, 0, :], logits, AX.X, ALU.max))
                then(eng.tensor_tensor(p_, logits, spread(0), ALU.subtract), "f_re")
                w(eng, "f_ree", 1)
                dl(eng.tensor_reduce(rt_s[:, 1, :], p_, AX.X, ALU.add))
                dl(eng.reciprocal(rt_s[:, 2, :], rt_s[:, 1, :]))
                dl(eng.tensor_tensor(p_, p_, spread(2), ALU.mult))
                for t in range(T):
                    last = eng.max(rt_8[:, t, :], rt_w[:, t, :])
                dl(last)
                dl(eng.memset(rt_8[:, :, K:8], -1.0))
                for t in range(T):
                    last = eng.match_replace(out=rt_o[:, t, :], in_to_replace=rt_8[:, t, :],
                                             in_values=rt_w[:, t, :], imm_value=0.0)
                dl(last)
                ins = eng.tensor_tensor(rt_c[:, :, 0:E], p_, rt_o[:, :, 0:E], ALU.subtract)
                if f == 0:
                    dl(ins)
                    dl(eng.tensor_reduce(rt_s[:, 1, :], rt_c[:, :, 0:E], AX.X, ALU.add))
                    dl(eng.reciprocal(rt_s[:, 2, :], rt_s[:, 1, :]))
                    dl(eng.tensor_tensor(rt_c[:, :, 0:E], rt_c[:, :, 0:E], spread(2), ALU.mult))
                    dl(eng.tensor_scalar(rt_c[:, :, E], rt_c[:, :, E], 1.0, None, ALU.add))
                    ins = eng.reciprocal(rt_c[:, :, E], rt_c[:, :, E])
                then(ins, "f_cb")
                for i in range(2):
                    cols = slice(i * HALF, (i + 1) * HALF)
                    w(eng, "f_cth", i + 1)
                    then(eng.tensor_tensor(combine_t[32:32 + EC, cols], psum[0:EC, 1 + i, :],
                                           combine_t[0:EC, cols].bitcast(F32), ALU.subtract), "f_ctd")

            if sign:
                relu(0, 0, 0, 0)
                relu(1, 1, 0, 0)
                half_lo(0, 0)
            else:
                route()
                gated(0, 0)
                weighted(0, 0)
                gated(1, 1)
                half_lo(0, 0)
                weighted(1, 1)

            def step(tile, slot, j):
                for hf in range(2):
                    n = tile * 2 + hf
                    half_lo(n - 1, 1 - hf)
                    if sign:
                        relu(n, hf, tile, slot)
                    else:
                        gated(n, hf)
                        weighted(n, hf)

            over_tiles(eng, step)
            half_lo(N - 1, 1)
            for t in range(T):
                w(eng, "f_dd", N - 1 if t < 4 else N)
                xt_ = x[:, t, :]
                if sign:
                    dl(eng.tensor_tensor(o_n[:, t % 2, :], acc(t), rows[:, 2, :], ALU.mult))
                    ins = eng.scalar_tensor_tensor(xt_, o_n[:, t % 2, :], scal[:, 2:3], xt_, ALU.mult, ALU.add)
                else:
                    ins = eng.scalar_tensor_tensor(xt_, acc(t), g_all[:, 4 + f:5 + f], xt_, ALU.mult, ALU.add)
                then(ins, "f_acc")
            w(eng, "f_acc", T)

        width = SW if sign else BW

        def load_tile(eng, blocks, tile, slot):
            if not isinstance(tile, int) or tile > 1:
                w(eng, "f_w2h" if sign else "f_w2r", tile - 1)
            eng.dma_start(ff_raw[:, slot, 0:width], blocks[bass.ds(tile, 1), :, :].rearrange(
                "one p c -> p (one c)")).then_inc(sems[f"d_ff{slot}"], 16)

        def sp_first(eng, blocks):
            for tile in range(2):
                load_tile(eng, blocks, tile, tile)

        def sp(eng, blocks):
            def load(tile, slot, j):
                load_tile(eng, blocks, tile, slot)

            pairs = (tiles - 2) // 2
            with eng.Fori(0, pairs) as i:
                load(i * 2 + 2, 0, i + 1)
                load(i * 2 + 3, 1, i + 1)
            if tiles % 2:
                load(tiles - 1, 0, tiles // 2)

        return pe, act, pool, dve, sp, early, sp_first

    def memory_pe(eng):
        eng.wait_ge(sems["f_acc"], T)
        def turn_x(b):
            wait(eng, "c_xn", b + 1)
            wait(eng, "c_lo", b)
            for c in range(KC):
                for qt in range(QT):
                    last = eng.transpose(psum[:, 3, c * S + qt * P:c * S + (qt + 1) * P],
                                         xn[:, qt, c * P:(c + 1) * P], ident)
            then(last, "c_xt")

        def scores(i):
            b, qt = divmod(i, QT)
            wait(eng, "c_lo", b + 1)
            wait(eng, "c_pn", i - 1)
            dst = psum[:, 4 + i % 2, :]
            passes(eng, dst, [lambda c: xt_hi[:, c, qt * P:(qt + 1) * P],
                              lambda c: xt_lo[:, c, qt * P:(qt + 1) * P]],
                   [lambda c: ctx_hi[:, c, b * M:(b + 1) * M], lambda c: ctx_lo[:, c, b * M:(b + 1) * M]],
                   stop=False)
            wait(eng, "c_mr", 1)
            r = 32 * b
            then(eng.matmul(dst, ones[r:r + 1, 0:P], mask_row[r:r + 1, :], start=False, stop=True,
                            skip_group_check=True, tile_position=(r, 0)), "c_sf")

        def turn_p(i):
            wait(eng, "c_pn", i + 1)
            wait(eng, "c_tl", i - 1)
            for kt in range(KT):
                last = eng.transpose(psum[:, 6 + i % 2, kt * P:(kt + 1) * P],
                                     pn[:, i % 2, kt * P:(kt + 1) * P], ident)
            then(last, "c_tf")

        def weigh(i):
            b = i // QT
            wait(eng, "q_tc", 2)
            wait(eng, "c_tl", i + 1)
            wait(eng, "c_cnl", b + 1)
            wait(eng, "c_x", i - 1)
            then(passes(eng, psum[:, i % 2, 0:D],
                        [lambda c: pt_hi[:, i % 2, c, :], lambda c: pt_lo[:, i % 2, c, :]],
                        [lambda c: cn_hi[:, b % 2, c, :], lambda c: cn_lo[:, b % 2, c, :]],
                        groups=KT), "c_pv")

        turn_x(0)
        eng.wait_ge(sems["q_int"], 1)
        for m in range(2):
            for c in range(KC):
                for r in range(2):
                    last = eng.transpose(psum[:, m, c * D + r * P:c * D + (r + 1) * P],
                                         w2_nat[:, m, r, c * P:(c + 1) * P], ident)
            then(last, "q_t")
        eng.wait_ge(sems["q_diag"], 1)
        for j in range(4):
            last = eng.matmul(psum[:, 2, j * P:(j + 1) * P], ones[:, 0:P].bitcast(F32), w2_diag[:, j, :],
                              start=True, stop=True, skip_group_check=True)
        then(last, "q_sp")
        for i in range(T + 2):
            if i < T:
                scores(i)
            if i % 2 and (i + 1) // 2 < B:
                turn_x((i + 1) // 2)
            if 1 <= i <= T:
                turn_p(i - 1)
            if i >= 2:
                weigh(i - 2)

    def memory_act(eng):
        def x_hi(b):
            wait(eng, "c_xt", b + 1)
            then(eng.activation(xt_hi[:, :, :].rearrange("p c t -> p (c t)"), psum[:, 3, :], ACT.Copy), "c_hi")

        def context_hi(b):
            eng.wait_ge(sems[f"d_cn{b % 2}"], 16 * (b // 2 + 1))
            if b == 0:
                eng.wait_ge(sems["f_dd"], 2 * TILES[0])
            wait(eng, "c_pv", QT * (b - 1))
            then(eng.activation(cn_hi[:, b % 2], cn_raw[:, b % 2], ACT.Copy), "c_cnh")

        x_hi(0)
        context_hi(0)
        for i in range(T + 1):
            if i < T:
                wait(eng, "c_mx", i + 1)
                wait(eng, "c_tf", i - 1)
                then(eng.activation(pn[:, i % 2, :], psum[:, 4 + i % 2, :], ACT.Exp, scale=1.0 / 16.0,
                                    bias=small[:, 2 * (i % 2):2 * (i % 2) + 1],
                                    accum_out=small[:, 2 * (i % 2) + 1:2 * (i % 2) + 2]), "c_pn")
            if i % 2 and (i + 1) // 2 < B:
                x_hi((i + 1) // 2)
            if i:
                wait(eng, "c_tf", i)
                wait(eng, "c_pv", i - 2)
                then(eng.activation(pt_hi[:, (i - 1) % 2].rearrange("p c t -> p (c t)"),
                                    psum[:, 6 + (i - 1) % 2, :], ACT.Copy), "c_th")
            if i % 2 and (i + 1) // 2 < B:
                context_hi((i + 1) // 2)

    def memory_pool(eng):
        for b in range(B):
            wait(eng, "c_pin", b + 1)
            then(eng.tensor_tensor(rstd[:, 0:QT], ve[:, 0:QT], half_neg[:, 0:QT], ALU.pow), "c_pout")

    def memory_dve(eng):
        def dl(ins):
            link(eng, "dve", ins)

        def ln(b):
            wait(eng, "c_xt", b)
            for qt in range(QT):
                last = eng.bn_stats(stat[:, qt, :], x[:, QT * b + qt, :])
            dl(last)
            for qt in range(QT):
                last = eng.bn_aggr(mv[:, qt, :], stat[:, qt, :])
            dl(last)
            then(eng.tensor_scalar(ve[:, 0:QT], mv[:, 0:QT, 1], LN_EPS, None, ALU.add), "c_pin")
            wait(eng, "c_pout", b + 1)
            for qt in range(QT):
                ins = eng.tensor_scalar(xn[:, qt, :], x[:, QT * b + qt, :], mv[:, qt, 0:1],
                                        rstd[:, qt:qt + 1], ALU.subtract, ALU.mult)
            then(ins, "c_xn")

        def x_lo(b):
            wait(eng, "c_hi", b + 1)
            then(eng.tensor_tensor(xt_lo[:, :, :].rearrange("p c t -> p (c t)"), psum[:, 3, :],
                                   xt_hi[:, :, :].rearrange("p c t -> p (c t)").bitcast(F32), ALU.subtract),
                 "c_lo")

        def context_lo(b):
            wait(eng, "c_cnh", b + 1)
            then(eng.tensor_tensor(cn_lo[:, b % 2], cn_raw[:, b % 2], cn_hi[:, b % 2].bitcast(F32),
                                   ALU.subtract), "c_cnl")

        ln(0)
        eng.wait_ge(sems["d_mask1"], 16)
        for b in range(B):
            r = slice(32 * b, 32 * b + 1)
            last = eng.tensor_scalar(mask_row[r, :], mask_u8[r, b, :], -1.0, -FAR, ALU.add, ALU.mult)
        then(last, "c_mr")
        x_lo(0)
        dl(eng.tensor_reduce(small[:, 8:8 + B], mask_u8[:, :, :], AX.X, ALU.max))
        dl(eng.tensor_scalar(small[:, 8:8 + B], small[:, 8:8 + B], g_all[:, 1:2], None, ALU.mult))
        context_lo(0)
        eng.wait_ge(sems["d_w2n"], 16)
        flat = w2_nat[:, :, :, :].rearrange("p m r c -> p (m r) c")
        dl(eng.tensor_reduce(small[:, 16:20], flat, AX.X, ALU.max, apply_absolute_value=True))
        dl(eng.tensor_scalar(small[:, 16:20], small[:, 16:20], 1.0 / 127.0, 1e-8, ALU.mult, ALU.max))
        dl(eng.reciprocal(small[:, 20:24], small[:, 16:20]))
        for j in range(4):
            ins = eng.tensor_scalar(flat[:, j, :], flat[:, j, :], small[:, 20 + j:21 + j], MAGIC,
                                    ALU.mult, ALU.add)
        dl(ins)
        then(eng.tensor_scalar(flat, flat, -MAGIC, 127.0, ALU.add, ALU.min), "q_int")
        for j in range(4):
            ins = eng.tensor_scalar(w2_diag[:, j, :], ident, small[:, 16 + j:17 + j], None, ALU.mult)
        then(ins, "q_diag")
        for m, mat in enumerate((WQ, WO)):
            wait(eng, "q_t", m + 1)
            then(eng.tensor_scalar(w_hi[:, mat].rearrange("p c n -> p (c n)"), psum[:, m, :], -127.0, None,
                                   ALU.max), "q_tc")
        wait(eng, "q_sp", 1)
        dl(eng.tensor_copy(w2_spread[:, :, :].rearrange("p m n -> p (m n)"), psum[:, 2, :]))

        for i in range(T + 2):
            if i < T:
                wait(eng, "c_sf", i + 1)
                m = small[:, 2 * (i % 2):2 * (i % 2) + 1]
                wait(eng, "c_pn", i - 1)
                dl(eng.tensor_reduce(m, psum[:, 4 + i % 2, :], AX.X, ALU.max, negate=True))
                then(eng.tensor_scalar(m, m, 1.0 / 16.0, None, ALU.mult), "c_mx")
            b1 = i // 2 + 1
            if b1 < B and i % 2 == 0:
                ln(b1)
            if b1 < B and i % 2:
                x_lo(b1)
            if 1 <= i <= T:
                wait(eng, "c_th", i)
                then(eng.tensor_tensor(pt_lo[:, (i - 1) % 2].rearrange("p c t -> p (c t)"),
                                       psum[:, 6 + (i - 1) % 2, :],
                                       pt_hi[:, (i - 1) % 2].rearrange("p c t -> p (c t)").bitcast(F32),
                                       ALU.subtract), "c_tl")
                j = (i - 1) % 2
                inv = small[:, 4 + j:5 + j]
                wait(eng, "c_pn", i)
                wait(eng, "c_x", i - 2)
                dl(eng.reciprocal(inv, small[:, 2 * j + 1:2 * j + 2]))
                b = (i - 1) // QT
                dl(eng.tensor_tensor(inv, inv, small[:, 8 + b:9 + b], ALU.mult))
            if b1 < B and i % 2:
                context_lo(b1)
            if i >= 2:
                t = i - 2
                wait(eng, "c_pv", t + 1)
                then(eng.scalar_tensor_tensor(x[:, t, :], psum[:, t % 2, 0:D], small[:, 4 + t % 2:5 + t % 2],
                                              x[:, t, :], ALU.mult, ALU.add), "c_x")
        wait(eng, "c_x", T)

    heads0, heads2, heads3 = attention(0), attention(2), attention(3)
    ff = [feed_forward(f) for f in range(4)]

    def attention_over(eng, blk, kind):
        eng.wait_ge(sems[kind], before_attention(kind, blk) + attention_events(kind, blk))


    block = ctx.enter_context(nc.Block())

    @block.sync
    def _(eng):
        def load(dst, src, name):
            eng.dma_start(dst, src).then_inc(sems[name], 16)

        def spread_row(dst, src, name):
            load(dst, src.rearrange("(one n) -> one n", one=1).to_broadcast([P, D]), name)

        x_rows = a["x"].rearrange("(b t p) n -> b p t n", p=P, t=QT)
        load(w_raw[:, WK], a["w0"][:, WK], "d_w01")
        load(ct_raw[:, 0], a["ctx_t"][:, :, 0:M], "d_ct0")
        load(ident_raw[:, :], a["ident"], "d_ident")
        load(consts[:, :], a["consts"], "d_ident")
        load(x[:, 0:QT, :], x_rows[0], "d_x0")
        eng.wait_ge(sems["z_done"], 1)
        for i, r in enumerate((0, 32, 64, 96)):
            load(bias_raw[r:r + 1, :, :], a["biases"][i // 2:i // 2 + 1, :, :], "d_bias")
        load(w_raw[:, WV], a["w0"][:, WV], "d_w02")
        load(w_raw[:, WQ], a["w0"][:, WQ], "d_w00")
        load(w_raw[:, WO], a["w0"][:, WO], "d_w03")
        for b in range(1, B):
            load(ct_raw[:, b], a["ctx_t"][:, :, b * M:(b + 1) * M], f"d_ct{b}")
            load(x[:, QT * b:QT * (b + 1), :], x_rows[b], f"d_x{b}")
        spread_row(rows[:, 0, :], a["L0_xattn_ln_gamma"], "d_rows0")
        spread_row(rows[:, 1, :], a["L0_xattn_ln_beta"], "d_rows0")
        spread_row(rows[:, 2, :], a["L2_ffn_down_scale"], "d_down")
        spread_row(rows[:, 3, :], a["L3_xattn_gk"], "d_rows3a")

        attention_over(eng, 0, "o_full")
        ff[0][6](eng, a["ff0"])
        attention_over(eng, 0, "b_done")
        load(gate_raw[:, :, :], a["gate0"], "d_gate")
        for m in (WK, WV):
            load(w_raw[:, m], a["w2"][:, m - 1], "d_w2")
        eng.wait_ge(sems["beta_used"], B)
        spread_row(rows[:, 0, :], a["L2_xattn_bq"], "d_rows2")
        spread_row(rows[:, 1, :], a["L2_xattn_bp"], "d_rows2")
        load(w2_nat[:, :, :, :], a["w2_nat"], "d_w2n")
        cn_rows = a["ctx"].rearrange("(b t p) n -> b p t n", p=P, t=KT)
        for b in range(2):
            load(cn_raw[:, b], cn_rows[b], f"d_cn{b}")
        ff[0][4](eng, a["ff0"])

        eng.wait_ge(sems["f_acc"], T)
        load(mask_u8[:, :, :], a["mask_row"].to_broadcast([P, B, M]), "d_mask1")
        ff[1][6](eng, a["ff1"])
        load(gate_raw[:, :, :], a["gate1"], "d_gate")
        for b in range(2, B):
            eng.wait_ge(sems["c_cnl"], b - 1)
            load(cn_raw[:, b % 2], cn_rows[b], f"d_cn{b % 2}")
        ff[1][4](eng, a["ff1"])

        attention_over(eng, 2, "o_full")
        ff[2][6](eng, a["ff2"])
        attention_over(eng, 2, "b_done")
        eng.wait_ge(sems["bp_used"], B)
        for m in (WK, WKI, WV, WVI, WQ, WO):
            load(w_raw[:, m], a["w3"][:, m], f"d_w3{m}")
        spread_row(rows[:, 0, :], a["L3_xattn_gk_img"], "d_rows3")
        spread_row(rows[:, 1, :], a["L3_xattn_gk"], "d_rows3")
        eng.wait_ge(sems["d_rows3a"], 16)
        load(rows[0:1, 3, :], a["L3_xattn_gk_img"].rearrange("(one n) -> one n", one=1), "d_rows3")
        ff[2][4](eng, a["ff2"])
        eng.wait_ge(sems["f_acc"], 3 * T)
        spread_row(rows[:, 2, :], a["L3_xattn_gq"], "d_rows3")

        attention_over(eng, 3, "o_full")
        ff[3][6](eng, a["ff3"])
        attention_over(eng, 3, "b_done")
        load(gate_raw[:, :, :], a["gate3"], "d_gate")
        ff[3][4](eng, a["ff3"])
        out_rows = out.rearrange("(t p) n -> t p n", p=P)
        for t in range(T):
            eng.wait_ge(sems["f_acc"], 3 * T + t + 1)
            load(out_rows[t], x[:, t, :], "d_out")
        eng.wait_ge(sems["d_out"], 16 * T)

    @block.gpsimd
    def _(eng):
        then(eng.memset(bias_raw[:, :, :], 0.0), "z_done")
        for dst, src in ((mask_i[:, :], a["mask_keys"]), (lens_i[:, :], a["lens"].to_broadcast([P, 1])),
                         (g_all[:, :], a["gates"].to_broadcast([P, 8])),
                         (scal[:, 0:1], a["residual_scale"].to_broadcast([P, 1])),
                         (scal[:, 1:2], a["output_scale"].to_broadcast([P, 1]))):
            eng.dma_start(dst, src).then_inc(sems["d_small"], 16)
        eng.memset(half_neg[:, :], -0.5)
        link(eng, "pool", eng.memset(values[:, :, :, :], 0.0))
        for buf in range(2):
            one = values[:, buf, 0:4, 0:NH * VW].rearrange("p s (h c) -> p s h c", c=VW)[:, :, :, HD]
            eng.memset(one, 1.0)
        eng.wait_ge(sems["d_ident"], 32)
        for buf in range(2):
            mixed = values[:, buf, 4, 0:NH * VW].rearrange("p (h c) -> p h c", c=VW)[:, :, HD]
            ins = eng.tensor_copy(mixed, not_img[:, 2:3].to_broadcast([P, NH]))
        then(ins, "v_init")
        def contexts_lo():
            for b in range(1, B):
                eng.wait_ge(sems["ct_h"], b + 1)
                cols = slice(b * M, (b + 1) * M)
                then(eng.tensor_tensor(ctx_lo[:, :, cols], ct_raw[:, b], ctx_hi[:, :, cols].bitcast(F32),
                                       ALU.subtract), "ct_l")

        heads0[2](eng, ff[0][5][1], contexts_lo)

        def split(mats, ready, done):
            for i, m in enumerate(mats):
                ready(i, m)
                link(eng, "pool", eng.tensor_copy(w_hi[:, m], w_raw[:, m]))
                then(eng.tensor_tensor(w_lo[:, m], w_raw[:, m], w_hi[:, m].bitcast(F32), ALU.subtract), done)

        ff[0][2](eng, extra=lambda: split((WK, WV), lambda i, m: eng.wait_ge(sems["d_w2"], 32), "w2_l"))
        memory_pool(eng)
        ff[1][5][1](eng)
        ff[1][2](eng)
        heads2[2](eng, ff[2][5][1])
        ff[2][2](eng, extra=lambda: split((WK, WKI, WV, WVI, WQ, WO),
                                          lambda i, m: eng.wait_ge(sems[f"d_w3{m}"], 16), "w3_l"))
        heads3[2](eng, ff[3][5][1])
        ff[3][2](eng)

    @block.scalar
    def _(eng):
        def w_part(m):
            eng.wait_ge(sems[f"d_w0{m}"], 16)
            then(eng.activation(w_hi[:, m], w_raw[:, m], ACT.Copy), "w0_h")

        def context(b):
            eng.wait_ge(sems[f"d_ct{b}"], 16)
            then(eng.activation(ctx_hi[:, :, b * M:(b + 1) * M], ct_raw[:, b], ACT.Copy), "ct_h")

        w_part(WK)
        context(0)
        eng.wait_ge(sems["d_bias"], 64)
        then(eng.activation(bias[:, :, :], bias_raw[:, :, :], ACT.Copy), "bias_h")
        w_part(WV)
        w_part(WQ)
        eng.wait_ge(sems["d_small"], 16 * 5)
        then(eng.activation(g_all[:, :], g_all[:, :], ACT.Tanh), "g_tanh")
        w_part(WO)
        for b in range(1, B):
            context(b)
        eng.wait_ge(sems["v_init"], 1)
        heads0[1](eng)
        ff[0][1](eng)
        memory_act(eng)
        ff[1][1](eng)
        heads2[1](eng)
        ff[2][1](eng)
        heads3[1](eng)
        ff[3][1](eng)

    @block.vector
    def _(eng):
        def w_part(n, m):
            eng.wait_ge(sems["w0_h"], n)
            then(eng.tensor_tensor(w_lo[:, m], w_raw[:, m], w_hi[:, m].bitcast(F32), ALU.subtract), "w0_l")

        then(eng.memset(ones[:, 0:P].bitcast(F32), 1.0), "ones_done")
        then(eng.memset(ones[:, P:2 * P].bitcast(F32), 0.0), "ones_done")
        eng.wait_ge(sems["d_ident"], 32)
        then(eng.tensor_copy(ident_r[:, :], ident_raw[:, :]), "ones_done")
        w_part(1, WK)
        eng.wait_ge(sems["ct_h"], 1)
        then(eng.tensor_tensor(ctx_lo[:, :, 0:M], ct_raw[:, 0], ctx_hi[:, :, 0:M].bitcast(F32), ALU.subtract),
             "ct_l0")
        eng.wait_ge(sems["bias_h"], 1)
        n0 = 4
        then(eng.tensor_tensor(bias[32:33, 0:n0], bias_raw[32:33, 0:n0], bias[32:33, 0:n0].bitcast(F32),
                               ALU.subtract), "bias_l")
        w_part(2, WV)

        def masks():
            eng.wait_ge(sems["d_small"], 16 * 5)
            link(eng, "dve", eng.tensor_scalar(aug0[:, :], mask_i[:, :], 0.5, 1.0, ALU.is_gt, ALU.subtract))
            link(eng, "dve", eng.tensor_scalar(aug0[:, :], aug0[:, :], -FAR, None, ALU.mult))
            lens, none = small[:, 0:1], small[:, 1:2]
            link(eng, "dve", eng.tensor_copy(lens, lens_i[:, :]))
            link(eng, "dve", eng.tensor_scalar(none, lens, 0.5, None, ALU.is_lt))
            keep = small[:, 4:8]
            link(eng, "dve", eng.tensor_scalar(keep, text_at, lens, none, ALU.is_lt, ALU.max))
            link(eng, "dve", eng.tensor_scalar(keep, keep, 1.0, -FAR, ALU.subtract, ALU.mult))
            eng.tensor_copy(aug3[:, :, 4], keep)
            for c in range(2):
                eng.tensor_copy(aug3[:, :, c], is_img)
                eng.tensor_copy(aug3[:, :, 2 + c], not_img)
            link(eng, "dve", eng.tensor_scalar(keep3[:, :], not_img, none, None, ALU.mult))
            then(eng.tensor_scalar(keep3[:, :], keep3[:, :], -1.0, 1.0, ALU.mult, ALU.add), "aug_done")
            eng.wait_ge(sems["aug_done"], 1)

        def matrices():
            w_part(3, WQ)
            w_part(4, WO)

        def biases_and_factors():
            then(eng.tensor_tensor(bias[32:33, n0:NB], bias_raw[32:33, n0:NB],
                                   bias[32:33, n0:NB].bitcast(F32), ALU.subtract), "bias_l")
            then(eng.tensor_tensor(bias[96:97], bias_raw[96:97], bias[96:97].bitcast(F32), ALU.subtract),
                 "bias_l")
            eng.wait_ge(sems["g_tanh"], 1)
            link(eng, "dve", eng.tensor_scalar(scal[:, 0:1], scal[:, 0:1], 0.0, 0.3, ALU.max, ALU.min))
            link(eng, "dve", eng.tensor_tensor(scal[:, 2:3], scal[:, 1:2], g_all[:, 6:7], ALU.mult))

        between = {("xt", 0): masks, ("st", 0, 0): matrices, ("st", 0, 1): biases_and_factors}
        eng.wait_ge(sems["d_x0"], 16)
        heads0[3](eng, ff[0][5][2], between)
        ff[0][3](eng)
        memory_dve(eng)
        ff[1][5][2](eng)
        ff[1][3](eng)
        eng.wait_ge(sems["d_rows2"], 32)
        heads2[3](eng, ff[2][5][2])
        eng.wait_ge(sems["d_down"], 16)
        ff[2][3](eng)
        eng.wait_ge(sems["d_rows3"], 64)
        heads3[3](eng, ff[3][5][2])
        ff[3][3](eng)

    @block.tensor
    def _(eng):
        eng.wait_ge(sems["ones_done"], 3)
        heads0[0](eng, ff[0][5][0])
        ff[0][0](eng)
        memory_pe(eng)
        ff[1][5][0](eng)
        ff[1][0](eng)
        heads2[0](eng, ff[2][5][0])
        ff[2][0](eng)
        heads3[0](eng, ff[3][5][0])
        ff[3][0](eng)

    ctx.close()


def kernel(**inputs):
    import concourse.bacc as bacc
    from concourse.bass_utils import run_bass_kernel_spmd

    v = {name: np.ascontiguousarray(value) for name, value in inputs.items()}

    def chunks(m):
        return m.reshape(KC, P, -1).transpose(1, 0, 2)

    def tiles_of(f, gate, up, down):
        n, spec = TILES[f], FFN[f]
        out = np.zeros((n, P, BW), np.float32)
        pad = n * P - UNITS[f]
        gate, up = (np.pad(m, ((0, 0), (0, pad))) for m in (gate, up))
        down = np.pad(down, ((0, pad), (0, 0)))
        owner = np.concatenate([np.repeat(np.arange(spec["E"]), spec["H"]), np.full(spec["HS"], spec["E"]),
                                np.full(pad, -1)])
        for t in range(n):
            cols = slice(t * P, (t + 1) * P)
            out[t, :, BG:BG + D] = chunks(gate[:, cols]).reshape(P, D)
            out[t, :, BU:BU + D] = chunks(up[:, cols]).reshape(P, D)
            out[t, :, BD:BD + D] = down[cols]
            select = (owner[None, cols] == np.arange(32)[:, None]).astype(np.float32)
            out[t, 0:32, BS:BS + P] = select
            out[t, 32:64, BS:BS + P] = select
        return out

    def units(m):
        return m.transpose(1, 0, 2).reshape(D, -1)

    arrays = {}
    arrays["x"] = v["x"].reshape(B * S, D)
    arrays["ctx"] = v["ctx_2048"].reshape(B * M, D)
    arrays["ctx_t"] = chunks(arrays["ctx"].T)
    arrays["w0"] = np.stack([chunks(v[f"L0_xattn_W{m}"].T) for m in "qkvo"], 1)
    wkv = v["L2_xattn_wkv"]
    arrays["w2"] = np.stack([chunks(wkv[0:D].T), chunks(wkv[D:2 * D].T)], 1)
    arrays["w2_nat"] = np.stack([chunks(v["L2_xattn_wq"]), chunks(v["L2_xattn_wp"])], 1)
    arrays["w3"] = np.stack([chunks(v[f"L3_xattn_W{m}"]) for m in ("q", "k", "v", "o", "k_img", "v_img")], 1)
    arrays["biases"] = np.stack([
        np.stack([v["L0_xattn_bq"], v["L0_xattn_bk"], v["L0_xattn_bv"], v["L0_xattn_bo"],
                  v["L2_xattn_bkv"][0:D], v["L2_xattn_bkv"][D:2 * D]]),
        np.stack([v[f"L3_xattn_b{m}"] for m in ("q", "k", "v", "o", "k_img", "v_img")])])
    key = np.arange(M).reshape(KT, P).T
    image = (key < IMG).astype(np.float32)
    arrays["ident"] = np.eye(P, dtype=np.float32)
    arrays["consts"] = np.concatenate([
        image, np.where(key < IMG, -2.0 ** 30, key - IMG).astype(np.float32),
        1 - image], 1)
    arrays["mask_keys"] = v["mask_BxS2_ik0"].reshape(B * KT, P).T
    arrays["mask_row"] = v["mask_BxS2_bk0"].reshape(1, B, M)
    arrays["lens"] = v["L3_xattn_context_lens"].reshape(1, 1)
    arrays["gates"] = np.concatenate([v["g_xattn"], v["g_ffn"]]).reshape(1, 8)
    arrays["residual_scale"] = v["L0_xattn_residual_scale"].reshape(1, 1)
    arrays["output_scale"] = v["L2_ffn_output_scale"].reshape(1, 1)
    for name in ("L0_xattn_ln_gamma", "L0_xattn_ln_beta", "L2_xattn_bq", "L2_xattn_bp", "L3_xattn_gq",
                 "L3_xattn_gk", "L3_xattn_gk_img", "L2_ffn_down_scale"):
        arrays[name] = v[name]
    gate0 = np.concatenate([v["L0_ffn_gate_w"].T, v["L0_ffn_shgate_w"][:, None]], 1)
    for f, m in ((0, gate0), (1, v["L1_ffn_router_w"]), (3, v["L3_ffn_gate_w"].T)):
        arrays[f"gate{f}"] = chunks(np.pad(m, ((0, 0), (0, 16 - m.shape[1]))))
    arrays["ff0"] = tiles_of(
        0, np.concatenate([units(v["L0_ffn_w_gate"]), v["L0_ffn_shw_gate"]], 1),
        np.concatenate([units(v["L0_ffn_w_up"]), v["L0_ffn_shw_up"]], 1),
        np.concatenate([v["L0_ffn_w_down"].reshape(-1, D), v["L0_ffn_shw_down"]], 0))
    arrays["ff1"] = tiles_of(
        1, np.concatenate([units(v["L1_ffn_w_gate"]), v["L1_ffn_shared_gate"]], 1),
        np.concatenate([units(v["L1_ffn_w_up"]), v["L1_ffn_shared_up"]], 1),
        np.concatenate([v["L1_ffn_w_down"].reshape(-1, D), v["L1_ffn_shared_down"]], 0))
    H3, HS3 = FFN[3]["H"], FFN[3]["HS"]
    w1, sw1 = v["L3_ffn_w1"].transpose(0, 2, 1), v["L3_ffn_shared_w1"].T
    arrays["ff3"] = tiles_of(
        3, np.concatenate([units(w1[:, :, 0:H3]), sw1[:, 0:HS3]], 1),
        np.concatenate([units(w1[:, :, H3:]), sw1[:, HS3:]], 1),
        np.concatenate([v["L3_ffn_w2"].transpose(0, 2, 1).reshape(-1, D), v["L3_ffn_shared_w2"].T], 0))
    up, down = v["L2_ffn_up_weight"].T, v["L2_ffn_down_weight"].T
    arrays["ff2"] = np.concatenate([
        up.reshape(KC, P, TILES[2], P).transpose(2, 1, 0, 3).reshape(TILES[2], P, D),
        down.reshape(TILES[2], P, D), v["L2_ffn_up_scale"].reshape(TILES[2], P, 1)], 2)

    nc = bacc.Bacc("TRN2", target_bir_lowering=False, num_devices=1)
    given, aps = {}, {}
    for name, value in arrays.items():
        value = np.ascontiguousarray(value)
        given[f"in_{name}"] = value
        aps[name] = nc.dram_tensor(f"in_{name}", value.shape, mybir.dt.from_np(value.dtype),
                                   kind="ExternalInput").ap()
    out = nc.dram_tensor("out", (B * S, D), F32, kind="ExternalOutput").ap()
    flamingo(nc, aps, out)
    r = run_bass_kernel_spmd(nc, [given], core_ids=[0])
    return r.results[0]["out"].reshape(B, S, D)
```
